# Optimizing a Trainium2 kernel written in Bass

```python
import numpy as np
import jax
import jax.numpy as jnp

def _softmax(x, axis=-1):
    return jax.nn.softmax(x, axis=axis)

def _gelu(x):
    return jax.nn.gelu(x, approximate=True)

def _silu(x):
    return jax.nn.silu(x)

def _sigmoid(x):
    return jax.nn.sigmoid(x)

def _layernorm(x, axis=-1, eps=1e-05):
    m = jnp.mean(x, axis=axis, keepdims=True)
    v = jnp.var(x, axis=axis, keepdims=True)
    return (x - m) / jnp.sqrt(v + eps)

def _scatter_add(tgt, idx, src, axis=0):
    return tgt.at[idx].add(src)

def _segment_sum(src, seg, n):
    return jax.ops.segment_sum(src, seg, n)
kernel_name = 'mk_seq_preln_d1_jaxref_r8_1e68a9'

def setup_inputs(seed: int=0):
    np.random.seed(seed)
    _w = jnp.asarray

    def _L0_attn_setup():
        import jax, jax.numpy as jnp
        import numpy as np
        D_MODEL, D_K, D_V, H = (128, 64, 64, 16)
        B, N = (2, 256)
        key = jax.random.key(seed)
        ks = jax.random.split(key, 5)
        y = jax.random.normal(ks[0], (B, N, D_MODEL), dtype=jnp.float32)
        Wq = 0.001 * jax.random.normal(ks[1], (H * D_K, D_MODEL), dtype=jnp.float32)
        Wk = 0.001 * jax.random.normal(ks[2], (H * D_K, D_MODEL), dtype=jnp.float32)
        Wv = 0.001 * jax.random.normal(ks[3], (H * D_V, D_MODEL), dtype=jnp.float32)
        Wo = 0.001 * jax.random.normal(ks[4], (D_MODEL, H * D_V), dtype=jnp.float32)
        bq = jnp.zeros((H * D_K,), jnp.float32)
        bk = jnp.zeros((H * D_K,), jnp.float32)
        bv = jnp.zeros((H * D_V,), jnp.float32)
        bo = jnp.zeros((D_MODEL,), jnp.float32)
        return {'y': y, 'Wq': Wq, 'bq': bq, 'Wk': Wk, 'bk': bk, 'Wv': Wv, 'bv': bv, 'Wo': Wo, 'bo': bo}
    _L0_attn_in = _L0_attn_setup()

    def _L0_ffn_setup():
        import jax, jax.numpy as jnp
        import numpy as np
        H_DIM, E_DIM = (128, 64)
        N_SHARED, N_ROUTED, TOP_K = (2, 16, 4)
        B, S = (4, 256)
        key = jax.random.key(seed)
        ks = jax.random.split(key, 6)
        sc = 1.0 / np.sqrt(H_DIM)
        ec = 1.0 / np.sqrt(E_DIM)
        return {'x': jax.random.normal(ks[0], (B, S, H_DIM), dtype=jnp.float32), 'shared_up': jax.random.uniform(ks[1], (N_SHARED, E_DIM, H_DIM), jnp.float32, -sc, sc), 'shared_down': jax.random.uniform(ks[2], (N_SHARED, H_DIM, E_DIM), jnp.float32, -ec, ec), 'routed_up': jax.random.uniform(ks[3], (N_ROUTED, E_DIM, H_DIM), jnp.float32, -sc, sc), 'routed_down': jax.random.uniform(ks[4], (N_ROUTED, H_DIM, E_DIM), jnp.float32, -ec, ec), 'router_w': jax.random.uniform(ks[5], (N_ROUTED, H_DIM), jnp.float32, -sc, sc)}
    _L0_ffn_in = _L0_ffn_setup()
    _d = {'L0_attn_y': _L0_attn_in['y'], 'L0_attn_Wq': _L0_attn_in['Wq'], 'L0_attn_bq': _L0_attn_in['bq'], 'L0_attn_Wk': _L0_attn_in['Wk'], 'L0_attn_bk': _L0_attn_in['bk'], 'L0_attn_Wv': _L0_attn_in['Wv'], 'L0_attn_bv': _L0_attn_in['bv'], 'L0_attn_Wo': _L0_attn_in['Wo'], 'L0_attn_bo': _L0_attn_in['bo'], 'L0_ffn_shared_up': _L0_ffn_in['shared_up'], 'L0_ffn_shared_down': _L0_ffn_in['shared_down'], 'L0_ffn_routed_up': _L0_ffn_in['routed_up'], 'L0_ffn_routed_down': _L0_ffn_in['routed_down'], 'L0_ffn_router_w': _L0_ffn_in['router_w']}
    _x0 = _d['L0_attn_y']
    _d['L0_attn_y'] = jax.random.normal(jax.random.fold_in(jax.random.key(seed), 1), (16, 512, 128), dtype=_x0.dtype)
    del _x0
    return _d

def reference(L0_attn_y, L0_attn_Wq, L0_attn_bq, L0_attn_Wk, L0_attn_bk, L0_attn_Wv, L0_attn_bv, L0_attn_Wo, L0_attn_bo, L0_ffn_shared_up, L0_ffn_shared_down, L0_ffn_routed_up, L0_ffn_routed_down, L0_ffn_router_w):

    def _L0_attn_ref(y, Wq, bq, Wk, bk, Wv, bv, Wo, bo):
        import jax, jax.numpy as jnp
        import numpy as np
        D_MODEL, D_K, D_V, H = (128, 64, 64, 16)
        B, N = (2, 256)
        b_s, n, _ = y.shape
        scale = 1.0 / np.sqrt(D_K).astype(np.float32)
        q = (jnp.einsum('bnd,ed->bne', y, Wq) + bq).reshape(b_s, n, H, D_K).transpose(0, 2, 1, 3)
        k = (jnp.einsum('bnd,ed->bne', y, Wk) + bk).reshape(b_s, n, H, D_K).transpose(0, 2, 1, 3)
        v = (jnp.einsum('bnd,ed->bne', y, Wv) + bv).reshape(b_s, n, H, D_V).transpose(0, 2, 1, 3)
        att = jnp.einsum('bhqd,bhkd->bhqk', q, k) * scale
        att = jax.nn.softmax(att, axis=-1)
        out = jnp.einsum('bhqk,bhkd->bhqd', att, v)
        out = out.transpose(0, 2, 1, 3).reshape(b_s, n, H * D_V)
        out = jnp.einsum('bne,de->bnd', out, Wo) + bo
        return out

    def _L0_ffn_ref(x, shared_up, shared_down, routed_up, routed_down, router_w):
        import jax, jax.numpy as jnp
        import numpy as np
        H_DIM, E_DIM = (128, 64)
        N_SHARED, N_ROUTED, TOP_K = (2, 16, 4)
        B, S = (4, 256)
        b, s, h = x.shape
        xt = x.reshape(-1, h)
        up_s = jnp.einsum('th,seh->tse', xt, shared_up)
        shared = jnp.einsum('tse,she->th', jax.nn.gelu(up_s, approximate=False), shared_down)
        probs = jax.nn.softmax(xt @ router_w.T, axis=-1)
        topk_p, topk_i = jax.lax.top_k(probs, TOP_K)
        gate = jnp.zeros_like(probs).at[jnp.arange(xt.shape[0])[:, None], topk_i].add(topk_p)
        up_r = jnp.einsum('th,reh->tre', xt, routed_up)
        act = jax.nn.gelu(up_r, approximate=False) * gate[:, :, None]
        routed = jnp.einsum('tre,rhe->th', act, routed_down)
        return (shared + routed).reshape(b, s, h)
    x = L0_attn_y
    x = x + _L0_attn_ref(_layernorm(x, axis=-1), L0_attn_Wq, L0_attn_bq, L0_attn_Wk, L0_attn_bk, L0_attn_Wv, L0_attn_bv, L0_attn_Wo, L0_attn_bo)
    x = x + _L0_ffn_ref(_layernorm(x, axis=-1), L0_ffn_shared_up, L0_ffn_shared_down, L0_ffn_routed_up, L0_ffn_routed_down, L0_ffn_router_w)
    return x

_drawn_inputs = setup_inputs


def setup_inputs(seed=0):
    import zlib

    import numpy as np

    out = dict(_drawn_inputs(seed))
    spreads = {'L0_attn_bq': (0.0, 2.0),
     'L0_attn_bk': (0.0, 2.0),
     'L0_attn_bv': (0.0, 0.8),
     'L0_attn_bo': (0.0, 0.1)}
    factors = {'L0_attn_Wq': 200.0, 'L0_attn_Wk': 64.0, 'L0_attn_Wv': 64.0, 'L0_attn_Wo': 8.0}
    for name, (base, spread) in spreads.items():
        noise = np.random.default_rng([zlib.crc32(name.encode()), seed]).standard_normal(out[name].shape)
        drawn = base * np.exp(spread * noise) if base else spread * noise
        out[name] = jnp.asarray(drawn.astype(out[name].dtype))
    for name, factor in factors.items():
        out[name] = (out[name] * factor).astype(out[name].dtype)
    return out
```

```python
from contextlib import ExitStack

import concourse.bass as bass
from concourse import mybir

ALU = mybir.AluOpType
ACT = mybir.ActivationFunctionType
AX = mybir.AxisListType
F32 = mybir.dt.float32
BF16 = mybir.dt.bfloat16
ds = bass.ds

P = 128
EPS = 1e-5
EULER = 2.718281828459045


def preln_layer(nc, y, Wq, bq, Wk, bk, Wv, bv, Wo, bo, s_up, s_dn, r_up, r_dn, r_w, out):
    B, N, D = y.shape
    NE = r_w.shape[0]
    DH = 64
    H = Wq.shape[0] // DH
    PAIRS = H // 2
    HALF = PAIRS // 2
    NB = N // P
    BLK = B * NB
    G = 2 * B
    SCALE = float(DH) ** -0.5
    CH = (s_up.shape[0] + NE) // 2
    RC = NE // 2
    TOP = 4
    assert D == P and N == 512 and NB == 4 and HALF == 4 and NE == 16 and CH == RC + 1

    CQ, CK, CV, CO = 0, PAIRS, 2 * PAIRS, 3 * PAIRS
    CU = 4 * PAIRS
    CD = CU + CH
    NW = CD + CH

    with ExitStack() as ctx:
        def sb(name, shape, dt):
            return ctx.enter_context(nc.sbuf_tensor(name, shape, dt))

        def pb(name, shape):
            return ctx.enter_context(nc.psum_tensor(name, shape, F32))

        def sem(name):
            return ctx.enter_context(nc.semaphore(name))

        ident = sb("ident", [P, P], F32)
        w_hi = sb("w_hi", [P, NW, P], BF16)
        w_lo = sb("w_lo", [P, NW, P], BF16)
        rw_nat = sb("rw_nat", [NE, P], F32)
        rw_hi = sb("rw_hi", [P, NE], BF16)
        rw_lo = sb("rw_lo", [P, NE], BF16)
        b_nat = sb("b_nat", [2 * PAIRS + 1, P], F32)
        b_col = sb("b_col", [P, 2 * PAIRS + 1], F32)
        bv_row = sb("bv_row", [P, H * DH], F32)
        yT_hi = sb("yT_hi", [P, B + 1, N], BF16)
        yT_lo = sb("yT_lo", [P, B + 1, N], BF16)
        accT = sb("accT", [P, B + 1, N], F32)
        w_nat = accT[:, :, :].rearrange("p a n -> p (a n)")[:, 0:NW * P].rearrange("p (c n) -> p c n", n=P)
        stack = sb("stack", [P, 4, 8, N], BF16)
        x_all = stack[:, :, :, :].rearrange("p a b n -> p (a b n)").bitcast(F32).rearrange("p (t d) -> p t d", d=D)
        KA0, KA1, QA0, QA1, KB0, KB1, QB0, QB1 = range(8)
        stats = sb("stats", [P, BLK, 6], F32)
        mean = sb("mean", [P, BLK], F32)
        rstd = sb("rstd", [P, BLK], F32)
        var = sb("var", [P, BLK], F32)
        tmp = sb("tmp", [P, BLK], F32)
        mhalf = sb("mhalf", [P, BLK], F32)
        euler = sb("euler", [P, NB * NE], F32)
        y32 = sb("y32", [P, 2, NB, D], F32)
        h_stage = sb("h_stage", [P, 2, N], BF16)
        l_stage = sb("l_stage", [P, 2, N], BF16)
        v32 = sb("v32", [P, H // 2 * DH], F32)
        vt = sb("vt", [P, 2, NB, H // 2, 129], BF16)
        mx = sb("mx", [P, 2, 8], F32)
        mrow = sb("mrow", [NB, P], BF16)
        p32 = sb("p32", [P, 4, N], F32)
        p_hi = sb("p_hi", [P, 2, NB, N], BF16)
        p_lo = sb("p_lo", [P, 2, NB, N], BF16)
        rden = sb("rden", [P, NB], F32)
        o_sb = sb("o_sb", [P, NB, P], F32)
        oT_hi = sb("oT_hi", [P, N], BF16)
        oT_lo = sb("oT_lo", [P, N], BF16)

        sel = sb("sel", [P, RC, P], BF16)
        sf = stack[:, :, :, :].rearrange("p a b n -> p (a b n)")
        gateT = sf[:, 0:2 * N].rearrange("p (a n) -> p a n", a=2)
        xT_hi = sf[:, 2 * N:4 * N].rearrange("p (a n) -> p a n", a=2)
        xT_lo = sf[:, 4 * N:6 * N].rearrange("p (a n) -> p a n", a=2)
        a_hi = sf[:, 6 * N:9 * N].rearrange("p (a n) -> p a n", a=3)
        a_lo = sf[:, 9 * N:12 * N].rearrange("p (a n) -> p a n", a=3)
        x1 = sf[:, 12 * N:16 * N].bitcast(F32).rearrange("p (a t d) -> p a t d", a=2, d=D)
        xr = sf[:, 16 * N:20 * N].bitcast(F32).rearrange("p (a t d) -> p a t d", a=2, d=D)
        o_st = sf[:, 20 * N:24 * N].bitcast(F32).rearrange("p (a t d) -> p a t d", a=2, d=D)
        f_sb = sf[:, 24 * N:26 * N].bitcast(F32)
        acc_st = sf[:, 28 * N:30 * N].bitcast(F32)
        xn = sf[:, 26 * N:28 * N].bitcast(F32).rearrange("p (t d) -> p t d", d=D)
        gl = p32
        a32 = p_hi[:, :, :, :].rearrange("p a b n -> p (a b n)")[:, 0:6 * N].bitcast(F32).rearrange("p (a n) -> p a n", a=3)
        rt = sb("rt", [P, 8, NB, NE], F32)
        top8 = sb("top8", [P, NB, 8], F32)
        rsm = sb("rsm", [P, 4, NB], F32)

        ps_s = pb("ps_s", [P, 2, N])
        ps_z = pb("ps_z", [P, 2, N])
        ps_o = pb("ps_o", [P, 2, N])
        ps_m = pb("ps_m", [P, 2, N])

        names = """ident selz zero const wload wload_o wload_u wload_r bload vload wT w_hi_ok w_lo_ok bT b_ok
            stats_ok chain rstd_ok y_ok yT yT_hi_ok yT_lo_ok acc_init ones_ok pinit
            proj hi_ok lo_ok stacked vproj v32_ok vhi_ok vlo_ok smax max_ok mT mrow_ok mrow_in
            scores exp_ok plo_ok pv rden_ok o_ok oT oTh_ok oTl_ok wo acc_ok
            attn_done c_acc c_accT c_x1 c_chain c_var c_rstd c_xn c_xT c_xTh c_xTl c_logit c_diff c_exp c_gate c_gT c_gh c_gl
            up gelu gbc act_ok ah_ok al_ok down f_ok fT out_ok""".split()
        S = {n: sem(n) for n in names}
        xload = [sem(f"xload{i}") for i in range(4)]
        xrl = [sem(f"xr_in{i}") for i in range(2)]
        st = [sem(f"stored{i}") for i in range(2)]

        block = ctx.enter_context(nc.Block())

        def n_exp(c): return c + 3
        def n_plo(c): return c + 5
        def n_pv(v): return v + 3
        def n_o(v): return v + 4
        def n_wo(x): return x + 3
        def n_acc(x): return x + 3
        def n_oT(x): return x + 2
        STK = 12 * 16

        def n_gelu(k): return k + 3
        def n_al(k): return k + 4
        def n_act(b, c): return b * RC + c + 2

        tok = "(t p) d -> p t d"

        @block.sync
        def _(sp):
            for w, c in ((Wq, CQ), (Wk, CK), (Wv, CV)):
                sp.dma_start(w_nat[:, c:c + PAIRS, :], w.rearrange("(c p) d -> p c d", p=P)).then_inc(S["wload"], 16)
            for i in range(4):
                for b in range(i * B // 4, (i + 1) * B // 4):
                    sp.dma_start(x_all[:, b * NB:(b + 1) * NB, :], y[b].rearrange(tok, p=P)).then_inc(xload[i], 16)

            def stack_moves(x, j, which):
                h, l, t = h_stage[:, which, :], l_stage[:, which, :], stack[:, j, :, :]
                hi_moves = ([(QA0, 0, 0), (QA0, 64, 0), (QA1, 0, 64), (QA1, 64, 64)] if which == 0 else
                            [(KA0, 0, 0), (KA1, 64, 64), (KB0, 0, 0), (KB1, 64, 64)])
                lo_moves = [(QB0, 0, 0), (QB1, 64, 64)] if which == 0 else [(KA0, 64, 0), (KA1, 0, 64)]
                sp.wait_ge(S["hi_ok"], 2 * x + which + 1)
                for col, to, of in hi_moves:
                    sp.dma_start(t[to:to + 64, col, :], h[of:of + 64, :]).then_inc(S["stacked"], 16)
                sp.wait_ge(S["lo_ok"], 2 * x + which + 1)
                for col, to, of in lo_moves:
                    sp.dma_start(t[to:to + 64, col, :], l[of:of + 64, :]).then_inc(S["stacked"], 16)

            def max_row(x, j, h):
                sp.wait_ge(S["mrow_ok"], 2 * x + h + 1)
                dst = stack[64:65, j, QB0, :] if h == 0 else stack[0:1, j, QB1, :]
                sp.dma_start(dst.rearrange("o (t q) -> o t q", q=P), mrow[:, :]).then_inc(S["mrow_in"], 16)

            sp.wait_ge(S["ones_ok"], 2)
            for x in range(2):
                stack_moves(x, x, 0)
                stack_moves(x, x, 1)
            max_row(0, 0, 0)
            with sp.Fori(0, G) as g:
                for j in range(HALF):
                    p = g * HALF + j
                    stack_moves(p + 2, (j + 2) % 4, 0)
                    max_row(p, j, 1)
                    stack_moves(p + 2, (j + 2) % 4, 1)
                    max_row(p + 1, (j + 1) % 4, 0)

            sp.wait_ge(S["attn_done"], 1)
            for par in range(2):
                sp.sem_inc(st[par], 16)
                sp.dma_start(xr[:, par, :, :], y[par].rearrange(tok, p=P)).then_inc(xrl[par], 16)
            with sp.Fori(0, B // 2) as i:
                for par in range(2):
                    b = i * 2 + par
                    sp.wait_ge(S["c_x1"], b + 1)
                    sp.dma_start(xr[:, par, :, :], y[ds((b + 2) % B, 1)].rearrange("o (t p) d -> p (o t) d", p=P)).then_inc(xrl[par], 16)
                    sp.wait_ge(S["out_ok"], b + 2)
                    sp.dma_start(out[ds(b, 1)].rearrange("o (t p) d -> p (o t) d", p=P), o_st[:, par, :, :]).then_inc(st[par], 16)
            for par in range(2):
                sp.wait_ge(st[par], 16 * (B // 2 + 1))
                sp.wait_ge(xrl[par], 16 * (B // 2 + 1))

        @block.gpsimd
        def _(pool):
            nc.gpsimd.memset(ident[:, :], 0.0).then_inc(S["ident"], 1)
            pool.wait_ge(S["ident"], 1)
            nc.gpsimd.affine_select(out=ident[:, :], in_=ident[:, :], compare_op=ALU.not_equal, fill=1.0, base=0,
                                    pattern=[[-1, P]], channel_multiplier=1).then_inc(S["ident"], 1)
            nc.gpsimd.memset(mhalf[:, :], -0.5)
            nc.gpsimd.memset(euler[:, :], EULER).then_inc(S["const"], 1)
            nc.gpsimd.memset(vt[:, :, :, :, :], 1.0)
            nc.gpsimd.memset(p_hi[:, :, :, :], 1.0)
            nc.gpsimd.memset(p_lo[:, :, :, :], 0.0)
            nc.gpsimd.memset(yT_hi[:, B, :], 0.0)
            nc.gpsimd.memset(yT_lo[:, B, :], 0.0)
            nc.gpsimd.memset(o_sb[:, :, :], 0.0).then_inc(S["pinit"], 1)
            nc.gpsimd.memset(sel[:, :, :], 0.0).then_inc(S["selz"], 1)
            v = sel[:, :, :].rearrange("p c (h l) -> p c h l", h=2)
            for k, base in enumerate((0, -32)):
                pool.wait_ge(S["selz"], k + 1)
                nc.gpsimd.affine_select(out=v, in_=v, compare_op=ALU.not_equal, fill=1.0, base=base,
                                        pattern=[[-2, RC], [-1, 2], [0, 64]], channel_multiplier=1).then_inc(S["selz"], 1)
            pool.sem_inc(S["plo_ok"], 4)
            pool.wait_ge(S["w_lo_ok"], WGROUPS)
            nc.gpsimd.memset(accT[:, :, :], 0.0).then_inc(S["acc_init"], 1)
            pool.wait_ge(S["stats_ok"], 1)
            nc.gpsimd.tensor_tensor(rstd[:, :], var[:, :], mhalf[:, :], ALU.pow).then_inc(S["rstd_ok"], 1)
            pool.wait_ge(S["y_ok"], B)
            nc.gpsimd.memset(stack[:, :, KB0:QB1 + 1, :], 0.0).then_inc(S["ones_ok"], 1)
            pool.wait_ge(S["ones_ok"], 1)
            nc.gpsimd.memset(stack[64:65, :, KB0, :], 1.0)
            nc.gpsimd.memset(stack[0:1, :, KB1, :], 1.0).then_inc(S["ones_ok"], 1)

            def v_lo(G1, kc, buf):
                pool.wait_ge(S["vhi_ok"], G1 * NB + kc + 1)
                dst = vt[:, ds(buf, 1), kc, :, :].rearrange("p o h c -> p (o h) c")
                nc.gpsimd.tensor_tensor(dst[:, :, 65:129], v32[:, :].rearrange("p (h c) -> p h c", c=DH),
                                        dst[:, :, 0:64], ALU.subtract).then_inc(S["vlo_ok"], 1)

            for kc in range(NB):
                v_lo(0, kc, 0)
            with pool.Fori(0, G) as g:
                for j in range(HALF):
                    p = g * HALF + j
                    for s in range(8):
                        h, kc = s // 4, s % 4
                        pool.wait_ge(S["exp_ok"], n_exp(p * 8 + s))
                        nc.gpsimd.tensor_tensor(p_lo[:, h, kc, :], p32[:, s % 4, :], p_hi[:, h, kc, :],
                                                ALU.subtract).then_inc(S["plo_ok"], 1)
                        if s == 4:
                            v_lo(g + 1, j, (g + 1) % 2)

            pool.wait_ge(S["attn_done"], 1)
            nc.gpsimd.memset(gateT[:, :, :], 0.0).then_inc(S["zero"], 1)

            def rstd_of(n):
                pool.wait_ge(S["c_var"], n + 1)
                nc.gpsimd.tensor_tensor(rsm[:, 1, :], rsm[:, 0, :], mhalf[:, 0:NB], ALU.pow).then_inc(S["c_rstd"], 1)

            def exp_of(n):
                pool.wait_ge(S["c_diff"], n + 1)
                nc.gpsimd.tensor_tensor(rt[:, 1, :, :].rearrange("p a b -> p (a b)"), euler[:, :],
                                        rt[:, 0, :, :].rearrange("p a b -> p (a b)"), ALU.pow).then_inc(S["c_exp"], 1)

            pool.sem_inc(S["al_ok"], 3)
            rstd_of(0)
            exp_of(0)
            with pool.Fori(0, B // 2) as i:
                for par in range(2):
                    b = i * 2 + par
                    for c in range(CH):
                        k = b * CH + c
                        pool.wait_ge(S["ah_ok"], k + 1)
                        src = gl[:, 0, :] if c == 0 else a32[:, c % 3, :]
                        nc.gpsimd.tensor_tensor(a_lo[:, c % 3, :], src, a_hi[:, c % 3, :], ALU.subtract).then_inc(S["al_ok"], 1)
                        if c == 2:
                            rstd_of(b + 1)
                        if c == 5:
                            exp_of(b + 1)

        @block.scalar
        def _(act):
            act.dma_start(b_nat[0:PAIRS, :], bq.rearrange("(c p) -> c p", p=P)).then_inc(S["bload"], 16)
            act.dma_start(b_nat[PAIRS:2 * PAIRS, :], bk.rearrange("(c p) -> c p", p=P)).then_inc(S["bload"], 16)
            act.dma_start(b_nat[2 * PAIRS:2 * PAIRS + 1, :], bo.rearrange("(c p) -> c p", p=P)).then_inc(S["bload"], 16)
            act.dma_start(rw_nat[:, :], r_w).then_inc(S["bload"], 16)
            act.dma_start(w_nat[:, CO:CO + PAIRS, :], Wo.rearrange("d (c e) -> d c e", e=P)).then_inc(S["wload_o"], 16)
            act.dma_start(bv_row[:, :], bv.rearrange("(o n) -> o n", o=1).broadcast_to([P, H * DH])).then_inc(S["vload"], 16)
            act.dma_start(w_nat[:, CU:CU + 1, :], s_up.rearrange("(c s) e h -> (s e) c h", s=2)).then_inc(S["wload_u"], 16)
            act.dma_start(w_nat[:, CU + 1:CU + CH, :], r_up.rearrange("(c s) e h -> (s e) c h", s=2)).then_inc(S["wload_u"], 16)
            act.dma_start(w_nat[:, CD, :].rearrange("h (s e) -> h s e", s=2), s_dn.rearrange("s h e -> h s e")).then_inc(S["wload_r"], 16)
            act.dma_start(w_nat[:, CD + 1:CD + CH, :].rearrange("h c (s e) -> h (c s) e", s=2),
                          r_dn.rearrange("r h e -> h r e")).then_inc(S["wload_r"], 16)
            act.sem_inc(S["exp_ok"], 2)

            for k in range(WGROUPS):
                c0, n = 4 * k, min(4, NW - 4 * k)
                act.wait_ge(S["wT"], k + 1)
                act.activation(w_hi[:, c0:c0 + n, :], ps_s[:, k % 2, 0:n * P], ACT.Copy).then_inc(S["w_hi_ok"], 1)
            act.wait_ge(S["bT"], 1)
            act.activation(b_col[:, :], ps_m[:, 0, 0:2 * PAIRS + 1], ACT.Copy)
            act.activation(rw_hi[:, :], ps_m[:, 1, 0:NE], ACT.Copy).then_inc(S["b_ok"], 1)
            with act.Fori(0, B // 2) as i:
                for par in range(2):
                    b = i * 2 + par
                    act.wait_ge(S["yT"], b + 1)
                    act.activation(yT_hi[:, ds(b, 1), :].rearrange("p o n -> p (o n)"), ps_z[:, par, :], ACT.Copy).then_inc(S["yT_hi_ok"], 1)

            def hi_part(x, which, col):
                act.wait_ge(S["proj"], 2 * x + which + 1)
                act.activation(h_stage[:, which, :], ps_m[:, 0, :], ACT.Identity, bias=b_col[:, col]).then_inc(S["hi_ok"], 1)

            def v_hi(G1, kc, buf):
                act.wait_ge(S["v32_ok"], G1 * NB + kc + 1)
                dst = vt[:, ds(buf, 1), kc, :, 0:64].rearrange("p o h c -> p (o h) c")
                act.activation(dst, v32[:, :].rearrange("p (h c) -> p h c", c=DH), ACT.Copy).then_inc(S["vhi_ok"], 1)

            act.wait_ge(S["pinit"], 1)
            for x in range(2):
                for which in range(2):
                    if x > 0:
                        act.wait_ge(S["stacked"], STK * x)
                    hi_part(x, which, slice(PAIRS * which + x, PAIRS * which + x + 1))
            for kc in range(NB):
                v_hi(0, kc, 0)
            with act.Fori(0, G) as g:
                for j in range(HALF):
                    p = g * HALF + j
                    col = (g % 2) * HALF + j + 2 if j < 2 else ((g + 1) % 2) * HALF + j - 2
                    for s in range(8):
                        h, kc = s // 4, s % 4
                        c = p * 8 + s
                        act.wait_ge(S["scores"], c + 1)
                        act.wait_ge(S["plo_ok"], n_plo(c - 4))
                        act.activation(p32[:, s % 4, :], ps_s[:, s % 2, :], ACT.Exp, scale=SCALE)
                        if kc == 0:
                            act.wait_ge(S["pv"], n_pv(p * 2 + h - 2))
                        act.activation(p_hi[:, h, kc, :], ps_s[:, s % 2, :], ACT.Exp, scale=SCALE).then_inc(S["exp_ok"], 1)
                        if s == 0:
                            act.wait_ge(S["stacked"], (p + 2) * STK)
                            hi_part(p + 2, 0, ds(col, 1))
                        if s == 2:
                            hi_part(p + 2, 1, ds(col + PAIRS, 1))
                        if s == 4:
                            act.wait_ge(S["pv"], n_pv(g * 8 - 1))
                            v_hi(g + 1, j, (g + 1) % 2)
                        if s == 5:
                            act.wait_ge(S["oT"], n_oT(p - 1))
                            act.wait_ge(S["wo"], n_wo(p - 2))
                            act.activation(oT_hi[:, :], ps_m[:, 0, :], ACT.Copy).then_inc(S["oTh_ok"], 1)

            act.wait_ge(S["oT"], n_oT(G * HALF - 1))
            act.activation(oT_hi[:, :], ps_m[:, 0, :], ACT.Copy).then_inc(S["oTh_ok"], 1)

            def prep_acc(n, blk):
                if not isinstance(n, int) or n > 0:
                    act.wait_ge(S["c_accT"], n)
                act.activation(acc_st, accT[:, ds(blk, 1), :].rearrange("p o n -> p (o n)"), ACT.Identity,
                               bias=b_col[:, 2 * PAIRS:2 * PAIRS + 1]).then_inc(S["c_acc"], 1)

            def prep_act(n, par):
                act.wait_ge(S["c_xT"], n + 1)
                act.activation(xT_hi[:, par, :], ps_z[:, 1, :], ACT.Copy).then_inc(S["c_xTh"], 1)

            def gate_act(n, par):
                act.wait_ge(S["c_gT"], n + 1)
                act.activation(gateT[0:NE, par, :], ps_z[0:NE, 1, :], ACT.Copy).then_inc(S["c_gh"], 1)

            act.wait_ge(S["zero"], 1)
            prep_acc(0, 1)
            prep_act(0, 0)
            gate_act(0, 0)
            act.sem_inc(S["gelu"], 2)
            prep_acc(1, 2)
            with act.Fori(0, B // 2) as i:
                for par in range(2):
                    b = i * 2 + par
                    for c in range(CH):
                        k = b * CH + c
                        act.wait_ge(S["up"], k + 1)
                        act.wait_ge(S["al_ok"], n_al(k - 3))
                        act.activation(gl[:, c % 3, :], ps_s[:, (par + c) % 2, :], ACT.Gelu).then_inc(S["gelu"], 1)
                        if c == 0:
                            act.wait_ge(S["gelu"], n_gelu(k))
                            src = gl[:, 0, :]
                        else:
                            act.wait_ge(S["act_ok"], n_act(b, c))
                            src = a32[:, c % 3, :]
                        act.activation(a_hi[:, c % 3, :], src, ACT.Copy).then_inc(S["ah_ok"], 1)
                        if c == 4:
                            prep_act(b + 1, 1 - par)
                        if c == 8:
                            gate_act(b + 1, 1 - par)
                        if c == 6:
                            prep_acc(b + 2, (b + 2) % B + 1)
                    act.wait_ge(S["down"], k + 1)
                    act.activation(f_sb, ps_m[:, 0, :], ACT.Copy).then_inc(S["f_ok"], 1)

        @block.vector
        def _(dve):
            for k in range(WGROUPS):
                c0, n = 4 * k, min(4, NW - 4 * k)
                dve.wait_ge(S["w_hi_ok"], k + 1)
                nc.vector.tensor_tensor(w_lo[:, c0:c0 + n, :], ps_s[:, k % 2, 0:n * P].rearrange("p (c n) -> p c n", n=P),
                                        w_hi[:, c0:c0 + n, :], ALU.subtract).then_inc(S["w_lo_ok"], 1)
            dve.wait_ge(S["b_ok"], 1)
            nc.vector.tensor_tensor(rw_lo[:, :], ps_m[:, 1, 0:NE], rw_hi[:, :], ALU.subtract).then_inc(S["b_ok"], 1)

            for i in range(4):
                dve.wait_ge(xload[i], 16 * (B // 4))
                with dve.Fori(i * BLK // 4, (i + 1) * BLK // 4) as t:
                    nc.vector.bn_stats(stats[:, ds(t, 1), :].rearrange("p o s -> p (o s)"),
                                       x_all[:, ds(t, 1), :].rearrange("p o d -> p (o d)")).then_inc(S["chain"], 1)

            def mean_var(st6, mean_, var_, tmp_, link):
                me, qe, mo, qo = (st6[:, :, f] for f in (1, 2, 4, 5))
                nc.vector.tensor_tensor(mean_, me, mo, ALU.add)
                nc.vector.tensor_tensor(tmp_, me, mo, ALU.subtract)
                link(nc.vector.tensor_tensor(var_, qe, qo, ALU.add))
                nc.vector.tensor_scalar(mean_, mean_, 0.5, None, ALU.mult)
                nc.vector.tensor_scalar(var_, var_, 1.0 / D, EPS, ALU.mult, ALU.add)
                link(nc.vector.scalar_tensor_tensor(out=tmp_, in0=tmp_, scalar=0.25, in1=tmp_, op0=ALU.mult, op1=ALU.mult))
                return nc.vector.tensor_tensor(var_, var_, tmp_, ALU.add)

            links = [BLK]

            def link(ins):
                links[0] += 1
                ins.then_inc(S["chain"], 1)
                dve.wait_ge(S["chain"], links[0])

            dve.wait_ge(S["chain"], BLK)
            mean_var(stats[:, :, :], mean[:, :], var[:, :], tmp[:, :], link).then_inc(S["stats_ok"], 1)
            dve.wait_ge(S["rstd_ok"], 1)
            with dve.Fori(0, B // 2) as i:
                for par in range(2):
                    b = i * 2 + par
                    if par == 0:
                        dve.wait_ge(S["chain"], BLK + 2)
                    for t in range(NB):
                        blk = b * NB + t
                        ins = nc.vector.tensor_scalar(y32[:, par, t, :], x_all[:, ds(blk, 1), :].rearrange("p o d -> p (o d)"),
                                                      mean[:, ds(blk, 1)], rstd[:, ds(blk, 1)], ALU.subtract, ALU.mult)
                    ins.then_inc(S["y_ok"], 1)
                    dve.wait_ge(S["yT_hi_ok"], b + 1)
                    nc.vector.tensor_tensor(yT_lo[:, ds(b, 1), :].rearrange("p o n -> p (o n)"), ps_z[:, par, :],
                                            yT_hi[:, ds(b, 1), :].rearrange("p o n -> p (o n)"), ALU.subtract).then_inc(S["yT_lo_ok"], 1)

            def lo_part(x, which, col):
                dve.wait_ge(S["hi_ok"], 2 * x + which + 1)
                nc.vector.scalar_tensor_tensor(out=l_stage[:, which, :], in0=ps_m[:, 0, :], scalar=b_col[:, col],
                                               in1=h_stage[:, which, :], op0=ALU.add, op1=ALU.subtract).then_inc(S["lo_ok"], 1)

            def v_bias(G1, kc, half, first):
                dve.wait_ge(S["vproj"], G1 * NB + kc + 1)
                if not first:
                    dve.wait_ge(S["vlo_ok"], G1 * NB + kc)
                nc.vector.tensor_tensor(v32[:, :], ps_m[:, 1, :], bv_row[:, ds(half * 512, 512)], ALU.add).then_inc(S["v32_ok"], 1)

            def row_max(x, par, t):
                dve.wait_ge(S["smax"], x * 8 + t + 1)
                nc.vector.tensor_reduce(mx[:, par, t:t + 1], ps_z[:, t % 2, :], AX.X, ALU.max).then_inc(S["max_ok"], 1)

            def max_row(x, h, first=False):
                e = x * 2 + h
                dve.wait_ge(S["mT"], e + 1)
                if not first:
                    dve.wait_ge(S["mrow_in"], e * 16)
                nc.vector.tensor_scalar(mrow[:, :], ps_m[0:NB, 1, 0:P], -1.0, None, ALU.mult).then_inc(S["mrow_ok"], 1)

            def normalise(v, h):
                o = ps_o[:, h, 0:NB * 65].rearrange("p (t c) -> p t c", c=65)
                dve.wait_ge(S["pv"], n_pv(v))
                dve.wait_ge(S["o_ok"], n_o(v - 1))
                nc.vector.reciprocal(rden[:, :], o[:, :, 64]).then_inc(S["rden_ok"], 1)
                dve.wait_ge(S["rden_ok"], v + 2)
                nc.vector.tensor_tensor(o_sb[:, :, h * 64:h * 64 + 64], o[:, :, 0:64],
                                        rden[:, :].unsqueeze(2).broadcast_to([P, NB, 64]), ALU.mult).then_inc(S["o_ok"], 1)

            dve.sem_inc(S["o_ok"], 2)
            for x in range(2):
                for which in range(2):
                    if x > 0:
                        dve.wait_ge(S["stacked"], STK * x)
                    lo_part(x, which, slice(PAIRS * which + x, PAIRS * which + x + 1))
            dve.wait_ge(S["vload"], 16)
            for kc in range(NB):
                v_bias(0, kc, 0, kc == 0)
            for t in range(8):
                row_max(0, 0, t)
            max_row(0, 0, True)
            dve.sem_inc(S["acc_ok"], 1)
            dve.wait_ge(S["acc_init"], 1)
            with dve.Fori(0, G) as g:
                for j in range(HALF):
                    p = g * HALF + j
                    col = (g % 2) * HALF + j + 2 if j < 2 else ((g + 1) % 2) * HALF + j - 2
                    for s in range(8):
                        if s == 5:
                            max_row(p + 1, 0)
                        row_max(p + 1, (j + 1) % 2, s)
                        if s == 0:
                            lo_part(p + 2, 0, ds(col, 1))
                        if s == 1:
                            max_row(p, 1)
                        if s == 2:
                            lo_part(p + 2, 1, ds(col + PAIRS, 1))
                        if s == 3:
                            v_bias(g + 1, j, (g + 1) % 2, False)
                        if s == 4:
                            normalise(p * 2 - 1, 1)
                        if s == 6:
                            dve.wait_ge(S["oTh_ok"], n_oT(p - 1))
                            nc.vector.tensor_tensor(oT_lo[:, :], ps_m[:, 0, :], oT_hi[:, :], ALU.subtract).then_inc(S["oTl_ok"], 1)
                    normalise(p * 2, 0)
                    dve.wait_ge(S["wo"], n_wo(p - 1))
                    to = (g + 1) // 2 if j == 0 else g // 2 + 1
                    dst = accT[:, ds(to, 1), :].rearrange("p o n -> p (o n)")
                    nc.vector.tensor_tensor(dst, ps_m[:, 0, :], dst, ALU.add).then_inc(S["acc_ok"], 1)
            LAST = G * HALF - 1
            normalise(2 * LAST + 1, 1)
            dve.wait_ge(S["oTh_ok"], n_oT(LAST))
            nc.vector.tensor_tensor(oT_lo[:, :], ps_m[:, 0, :], oT_hi[:, :], ALU.subtract).then_inc(S["oTl_ok"], 1)
            dve.wait_ge(S["wo"], n_wo(LAST))
            nc.vector.tensor_tensor(accT[:, B, :], ps_m[:, 0, :], accT[:, B, :], ALU.add).then_inc(S["acc_ok"], 1)
            dve.wait_ge(S["acc_ok"], n_acc(LAST))

            CHAIN = 13

            def prep_x1(n, par, ln):
                dve.wait_ge(S["c_accT"], n + 1)
                dve.wait_ge(xrl[par], ln)
                nc.vector.tensor_tensor(x1[:, par, :, :].rearrange("p t d -> p (t d)"), ps_z[:, 0, :],
                                        xr[:, par, :, :].rearrange("p t d -> p (t d)"), ALU.add).then_inc(S["c_x1"], 1)
                dve.wait_ge(S["c_x1"], n + 1)

            def chain_from(n, k0):
                k = [k0]

                def link(ins):
                    k[0] += 1
                    ins.then_inc(S["c_chain"], 1)
                    dve.wait_ge(S["c_chain"], n * CHAIN + k[0])
                return link

            def prep_stats(n, par):
                link = chain_from(n, 0)
                for t in range(NB):
                    ins = nc.vector.bn_stats(stats[:, t, :], x1[:, par, t, :])
                link(ins)
                mean_var(stats[:, 0:NB, :], rsm[:, 2, :], rsm[:, 0, :], rsm[:, 3, :], link).then_inc(S["c_var"], 1)

            def prep_norm(n, par):
                dve.wait_ge(S["c_rstd"], n + 1)
                for t in range(NB):
                    ins = nc.vector.tensor_scalar(xn[:, t, :], x1[:, par, t, :], rsm[:, 2, t:t + 1], rsm[:, 1, t:t + 1],
                                                  ALU.subtract, ALU.mult)
                ins.then_inc(S["c_xn"], 1)

            def prep_xT(n, par):
                dve.wait_ge(S["c_xTh"], n + 1)
                nc.vector.tensor_tensor(xT_lo[:, par, :], ps_z[:, 1, :], xT_hi[:, par, :], ALU.subtract).then_inc(S["c_xTl"], 1)

            def wide(m):
                return m.unsqueeze(2).broadcast_to([P, NB, NE])

            def prep_diff(n):
                link = chain_from(n, 3)
                lg = ps_z[:, 0, 0:NB * NE].rearrange("p (t e) -> p t e", e=NE)
                dve.wait_ge(S["c_logit"], n + 1)
                link(nc.vector.tensor_reduce(rsm[:, 0, :], lg, AX.X, ALU.max))
                nc.vector.tensor_tensor(rt[:, 0, :, :], lg, wide(rsm[:, 0, :]), ALU.subtract).then_inc(S["c_diff"], 1)

            def prep_gate(n):
                link = chain_from(n, 4)
                e, gt, eq, pa, pc = (rt[:, k, :, :] for k in (1, 2, 3, 4, 5))
                dve.wait_ge(S["c_exp"], n + 1)
                nc.vector.tensor_reduce(rsm[:, 1, :], e, AX.X, ALU.add)
                for t in range(NB):
                    ins = nc.vector.max(top8[:, t, :], rt[:, 1, t, :])
                link(ins)
                thr = wide(top8[:, :, TOP - 1])
                nc.vector.tensor_tensor(gt, e, thr, ALU.is_gt)
                link(nc.vector.tensor_tensor(eq, e, thr, ALU.is_equal))
                nc.vector.reciprocal(rsm[:, 2, :], rsm[:, 1, :])
                link(nc.vector.tensor_reduce(rsm[:, 3, :], gt, AX.X, ALU.add))
                src, dst, step = eq, pa, 1
                while step < NE:
                    nc.vector.tensor_copy(dst[:, :, 0:step], src[:, :, 0:step])
                    link(nc.vector.tensor_tensor(dst[:, :, step:NE], src[:, :, step:NE], src[:, :, 0:NE - step], ALU.add))
                    src, dst, step = dst, (pc if dst is pa else pa), 2 * step
                link(nc.vector.tensor_tensor(dst, src, wide(rsm[:, 3, :]), ALU.add))
                link(nc.vector.scalar_tensor_tensor(out=src, in0=dst, scalar=float(TOP), in1=eq, op0=ALU.is_le, op1=ALU.mult))
                nc.vector.tensor_tensor(rt[:, 6, :, :], e, wide(rsm[:, 2, :]), ALU.mult)
                nc.vector.tensor_tensor(gt, gt, src, ALU.add).then_inc(S["c_gate"], 1)
                dve.wait_ge(S["c_gate"], n * 2 + 1)
                nc.vector.tensor_tensor(rt[:, 7, :, :], gt, rt[:, 6, :, :], ALU.mult).then_inc(S["c_gate"], 1)

            def prep_gT(n, par):
                dve.wait_ge(S["c_gh"], n + 1)
                nc.vector.tensor_tensor(gateT[32:32 + NE, par, :], ps_z[0:NE, 1, :], gateT[0:NE, par, :],
                                        ALU.subtract).then_inc(S["c_gl"], 1)

            prep_x1(0, 0, 16)
            prep_stats(0, 0)
            prep_norm(0, 0)
            prep_xT(0, 0)
            prep_diff(0)
            prep_gate(0)
            prep_gT(0, 0)
            dve.sem_inc(S["act_ok"], 2)
            dve.sem_inc(S["out_ok"], 1)
            with dve.Fori(0, B // 2) as i:
                for par in range(2):
                    b = i * 2 + par
                    n, np_ = b + 1, 1 - par
                    for c in range(CH):
                        k = b * CH + c
                        if c == 0:
                            dve.wait_ge(S["out_ok"], b + 1)
                            prep_x1(n, np_, (i + 1) * 16 if par == 0 else (i + 2) * 16)
                            prep_stats(n, np_)
                        else:
                            dve.wait_ge(S["gelu"], n_gelu(k))
                            dve.wait_ge(S["gbc"], b * RC + c)
                            nc.vector.tensor_tensor(a32[:, c % 3, :], gl[:, c % 3, :], ps_o[:, c % 2, :], ALU.mult).then_inc(S["act_ok"], 1)
                        if c == 3:
                            prep_norm(n, np_)
                        if c == 4:
                            prep_xT(n, np_)
                        if c == 5:
                            prep_diff(n)
                        if c == 7:
                            prep_gate(n)
                        if c == 8:
                            prep_gT(n, np_)
                    dve.wait_ge(S["fT"], b + 1)
                    dve.wait_ge(st[par], (i + 1) * 16)
                    nc.vector.tensor_tensor(o_st[:, par, :, :].rearrange("p t d -> p (t d)"), ps_m[:, 1, :],
                                            x1[:, par, :, :].rearrange("p t d -> p (t d)"), ALU.add).then_inc(S["out_ok"], 1)

        @block.tensor
        def _(pe):
            mm, tr = nc.tensor.matmul, nc.tensor.transpose

            def one(ap):
                return ap.rearrange("p o n -> p (o n)")

            pe.wait_ge(S["ident"], 2)
            for k in range(WGROUPS):
                c0, n = 4 * k, min(4, NW - 4 * k)
                last = c0 + n
                for nm, v, upto in (("wload", 48, 0), ("wload_o", 16, CO), ("wload_u", 32, CU), ("wload_r", 32, CD)):
                    if last > upto:
                        pe.wait_ge(S[nm], v)
                if k >= 2:
                    pe.wait_ge(S["w_lo_ok"], k - 1)
                for q in range(n):
                    ins = tr(ps_s[:, k % 2, q * P:(q + 1) * P], w_nat[:, c0 + q, :], ident[:, :])
                ins.then_inc(S["wT"], 1)
            pe.wait_ge(S["bload"], 64)
            tr(ps_m[:, 0, 0:2 * PAIRS + 1], b_nat[:, :], ident[0:2 * PAIRS + 1, 0:2 * PAIRS + 1])
            tr(ps_m[:, 1, 0:NE], rw_nat[:, :], ident[0:NE, 0:NE]).then_inc(S["bT"], 1)
            with pe.Fori(0, B // 2) as i:
                for par in range(2):
                    b = i * 2 + par
                    pe.wait_ge(S["y_ok"], b + 1)
                    for t in range(NB):
                        ins = tr(ps_z[:, par, t * P:(t + 1) * P], y32[:, par, t, :], ident[:, :])
                    ins.then_inc(S["yT"], 1)

            def three(dst, wh, wl, mh, ml):
                mm(dst, wh, mh, start=True, stop=False)
                mm(dst, wl, mh, start=False, stop=False)
                return mm(dst, wh, ml, start=False, stop=True)

            def project(chunk, yb):
                three(ps_m[:, 0, :], one(w_hi[:, ds(chunk, 1), :]), one(w_lo[:, ds(chunk, 1), :]),
                      one(yT_hi[:, ds(yb, 1), :]), one(yT_lo[:, ds(yb, 1), :])).then_inc(S["proj"], 1)

            def project_v(half, yb, kc):
                yh = yT_hi[:, ds(yb, 1), kc * P:(kc + 1) * P].rearrange("p o n -> p (o n)")
                yl = yT_lo[:, ds(yb, 1), kc * P:(kc + 1) * P].rearrange("p o n -> p (o n)")
                wh = w_hi[:, ds(half * HALF + CV, HALF), :].rearrange("p c n -> p (c n)")
                wl = w_lo[:, ds(half * HALF + CV, HALF), :].rearrange("p c n -> p (c n)")
                d = ps_m[:, 1, :]
                mm(d, yh, wh, start=True, stop=False)
                mm(d, yh, wl, start=False, stop=False)
                mm(d, yl, wh, start=False, stop=True).then_inc(S["vproj"], 1)

            def queries_scores(j, t):
                ka, qa = ((KA0, QA0), (KA1, QA1))[t // 4]
                q0 = (t % 4) * P
                mm(ps_z[:, t % 2, :], stack[:, j, qa, q0:q0 + P], stack[:, j, ka, :], start=True, stop=True).then_inc(S["smax"], 1)

            def turn_maxima(par, h):
                tr(ps_m[0:NB, 1, 0:P], mx[:, par, 4 * h:4 * h + 4], ident[:, :]).then_inc(S["mT"], 1)

            def pv_chunk(buf, hv, kc, h8):
                for t in range(NB):
                    q = slice(t * P, (t + 1) * P)
                    ph, pl = p_hi[:, hv, kc, q], p_lo[:, hv, kc, q]
                    vh = vt[:, ds(buf, 1), kc, h8, 0:65]
                    vl = vt[:, ds(buf, 1), kc, h8, 65:129]
                    d = ps_o[:, hv, t * 65:t * 65 + 65]
                    mm(d, ph, vh, start=(kc == 0 and t == 0), stop=False, skip_group_check=True)
                    mm(d[:, 0:64], ph, vl, start=False, stop=False, skip_group_check=True)
                    ins = mm(d, pl, vh, start=False, stop=(kc == NB - 1 and t == NB - 1), skip_group_check=True)
                return ins

            def turn_o():
                for t in range(NB):
                    ins = tr(ps_m[:, 0, t * P:(t + 1) * P], o_sb[:, t, :], ident[:, :])
                ins.then_inc(S["oT"], 1)

            def out_proj(chunk):
                three(ps_m[:, 0, :], one(w_hi[:, ds(chunk, 1), :]), one(w_lo[:, ds(chunk, 1), :]),
                      oT_hi[:, :], oT_lo[:, :]).then_inc(S["wo"], 1)

            pe.wait_ge(S["yT_lo_ok"], B)
            pe.wait_ge(S["pinit"], 1)
            pe.wait_ge(S["b_ok"], 2)
            for x in range(2):
                for which in range(2):
                    if 2 * x + which > 0:
                        pe.wait_ge(S["lo_ok"], 2 * x + which)
                    project(PAIRS * which + x, 0)
            for kc in range(NB):
                if kc > 0:
                    pe.wait_ge(S["v32_ok"], kc)
                project_v(0, 0, kc)
            pe.wait_ge(S["stacked"], STK)
            for t in range(8):
                if t > 1:
                    pe.wait_ge(S["max_ok"], t - 1)
                queries_scores(0, t)
            pe.wait_ge(S["max_ok"], 4)
            pe.wait_ge(S["v32_ok"], NB)
            turn_maxima(0, 0)
            pe.sem_inc(S["pv"], 1)
            pe.sem_inc(S["wo"], 1)
            with pe.Fori(0, G) as g:
                for j in range(HALF):
                    p = g * HALF + j
                    if j < 2:
                        chunk, yb = (g % 2) * HALF + j + 2, g // 2
                    else:
                        chunk, yb = ((g + 1) % 2) * HALF + j - 2, (g + 1) // 2
                    for s in range(8):
                        h, kc = s // 4, s % 4
                        ka, qa, kb, qb = ((KA0, QA0, KB0, QB0), (KA1, QA1, KB1, QB1))[h]
                        kk = slice(kc * P, (kc + 1) * P)
                        pe.wait_ge(S["exp_ok"], n_exp(p * 8 + s - 2))
                        mm(ps_s[:, s % 2, :], stack[:, j, ka, kk], stack[:, j, qa, :], start=True, stop=False)
                        if kc == 0:
                            pe.wait_ge(S["mrow_in"], (p * 2 + h + 1) * 16)
                        mm(ps_s[:, s % 2, :], stack[:, j, kb, kk], stack[:, j, qb, :], start=False, stop=True).then_inc(S["scores"], 1)
                        if s == 0:
                            pe.wait_ge(S["stacked"], (p + 2) * STK)
                        pe.wait_ge(S["max_ok"], (p + 1) * 8 + s - 1)
                        queries_scores((j + 1) % 4, s)
                        v = p * 2 + h - 1
                        if kc == 0:
                            pe.wait_ge(S["o_ok"], n_o(v - 2))
                        if j == 0 and s == 4:
                            pe.wait_ge(S["vlo_ok"], (g + 1) * NB)
                        pe.wait_ge(S["plo_ok"], n_plo(v * 4 + kc))
                        h8 = (2 * j + h - 1) % 8
                        buf = (g + 1) % 2 if j == 0 and h == 0 else g % 2
                        ins = pv_chunk(buf, 1 - h, kc, h8)
                        if kc == NB - 1:
                            ins.then_inc(S["pv"], 1)
                        if s == 0:
                            pe.wait_ge(S["acc_ok"], n_acc(p - 2))
                            project(chunk, yb)
                        if s == 1:
                            pe.wait_ge(S["max_ok"], p * 8 + 8)
                            pe.wait_ge(S["mrow_ok"], p * 2 + 1)
                            turn_maxima(j % 2, 1)
                        if s == 2:
                            pe.wait_ge(S["lo_ok"], (p + 2) * 2 + 1)
                            project(chunk + PAIRS, yb)
                        if s == 3:
                            pe.wait_ge(S["mrow_ok"], p * 2 + 2)
                            project_v((g + 1) % 2, (g + 1) // 2, j)
                        if s == 5:
                            pe.wait_ge(S["max_ok"], p * 8 + 12)
                            pe.wait_ge(S["v32_ok"], g * NB + NB + j + 1)
                            turn_maxima((j + 1) % 2, 0)
                            pe.wait_ge(S["o_ok"], n_o(p * 2 - 1))
                            pe.wait_ge(S["lo_ok"], (p + 2) * 2 + 2)
                            turn_o()
                        if s == 7:
                            pe.wait_ge(S["oTl_ok"], n_oT(p - 1))
                            out_proj(((g + 1) % 2) * HALF + (HALF - 1) + CO if j == 0 else (g % 2) * HALF + j - 1 + CO)
            LAST = G * HALF - 1
            pe.wait_ge(S["o_ok"], n_o(2 * LAST - 1))
            for kc in range(NB):
                pe.wait_ge(S["plo_ok"], n_plo((2 * LAST + 1) * 4 + kc))
                ins = pv_chunk((G - 1) % 2, 1, kc, 7)
            ins.then_inc(S["pv"], 1)
            pe.wait_ge(S["o_ok"], n_o(2 * LAST + 1))
            pe.wait_ge(S["acc_ok"], n_acc(LAST - 1))
            turn_o()
            pe.wait_ge(S["oTl_ok"], n_oT(LAST))
            out_proj(CO + PAIRS - 1)
            pe.wait_ge(S["acc_ok"], n_acc(LAST))
            pe.wait_ge(S["max_ok"], (LAST + 2) * 8)
            pe.wait_ge(S["vlo_ok"], (G + 1) * NB)
            pe.wait_ge(S["mrow_in"], (LAST * 2 + 3) * 16)
            pe.wait_ge(S["stacked"], (LAST + 3) * STK)
            pe.sem_inc(S["attn_done"], 1)

            def turn_acc(n, first=False):
                pe.wait_ge(S["c_acc"], n + 1)
                if not first:
                    pe.wait_ge(S["c_diff"], n)
                for t in range(NB):
                    ins = tr(ps_z[:, 0, t * P:(t + 1) * P], acc_st[:, t * P:(t + 1) * P], ident[:, :])
                ins.then_inc(S["c_accT"], 1)

            def turn_xn(n):
                pe.wait_ge(S["c_xn"], n + 1)
                for t in range(NB):
                    ins = tr(ps_z[:, 1, t * P:(t + 1) * P], xn[:, t, :], ident[:, :])
                ins.then_inc(S["c_xT"], 1)

            def route(n, par):
                pe.wait_ge(S["c_xTl"], n + 1)
                for t in range(NB):
                    q = slice(t * P, (t + 1) * P)
                    d = ps_z[:, 0, t * NE:(t + 1) * NE]
                    mm(d, xT_hi[:, par, q], rw_hi[:, :], start=True, stop=False)
                    mm(d, xT_hi[:, par, q], rw_lo[:, :], start=False, stop=False)
                    ins = mm(d, xT_lo[:, par, q], rw_hi[:, :], start=False, stop=True)
                ins.then_inc(S["c_logit"], 1)

            def turn_gates(n):
                pe.wait_ge(S["c_gate"], n * 2 + 2)
                for t in range(NB):
                    ins = tr(ps_z[0:NE, 1, t * P:(t + 1) * P], rt[:, 7, t, :], ident[:, :])
                ins.then_inc(S["c_gT"], 1)

            turn_acc(0, True)
            turn_xn(0)
            route(0, 0)
            turn_gates(0)
            pe.wait_ge(S["c_gl"], 1)
            with pe.Fori(0, B // 2) as i:
                for par in range(2):
                    b = i * 2 + par

                    def down(c):
                        k = b * CH + c
                        pe.wait_ge(S["al_ok"], n_al(k))
                        w = CD + c
                        mm(ps_m[:, 0, :], w_hi[:, w, :], a_hi[:, c % 3, :], start=(c == 0), stop=False)
                        mm(ps_m[:, 0, :], w_lo[:, w, :], a_hi[:, c % 3, :], start=False, stop=False)
                        mm(ps_m[:, 0, :], w_hi[:, w, :], a_lo[:, c % 3, :], start=False, stop=(c == CH - 1)).then_inc(S["down"], 1)

                    for c in range(CH):
                        if c == 0:
                            turn_acc(b + 1)
                        pe.wait_ge(S["gelu"], n_gelu(b * CH + c - 2))
                        three(ps_s[:, (par + c) % 2, :], w_hi[:, CU + c, :], w_lo[:, CU + c, :],
                              xT_hi[:, par, :], xT_lo[:, par, :]).then_inc(S["up"], 1)
                        if c > 0:
                            pe.wait_ge(S["act_ok"], n_act(b, c - 2))
                            mm(ps_o[:, c % 2, :], sel[:, c - 1, :], gateT[:, par, :], start=True, stop=True).then_inc(S["gbc"], 1)
                        if c >= 2:
                            down(c - 2)
                        if c == 4:
                            turn_xn(b + 1)
                        if c == 6:
                            route(b + 1, 1 - par)
                    down(CH - 2)
                    down(CH - 1)
                    turn_gates(b + 1)
                    pe.wait_ge(S["f_ok"], b + 1)
                    for t in range(NB):
                        ins = tr(ps_m[:, 1, t * P:(t + 1) * P], f_sb[:, t * P:(t + 1) * P], ident[:, :])
                    ins.then_inc(S["fT"], 1)
                    pe.wait_ge(S["c_gl"], b + 2)


WGROUPS = 13

_INS = ['L0_attn_y', 'L0_attn_Wq', 'L0_attn_bq', 'L0_attn_Wk', 'L0_attn_bk', 'L0_attn_Wv', 'L0_attn_bv', 'L0_attn_Wo',
        'L0_attn_bo', 'L0_ffn_shared_up', 'L0_ffn_shared_down', 'L0_ffn_routed_up', 'L0_ffn_routed_down', 'L0_ffn_router_w']


def kernel(**inputs):
    import numpy as _np
    import concourse.bacc as _bacc
    from concourse import mybir as _mybir
    from concourse.bass_utils import run_bass_kernel_spmd as _run

    nc = _bacc.Bacc("TRN2", target_bir_lowering=False, num_devices=1)
    arrays, args = {}, []
    for name in _INS:
        a = _np.ascontiguousarray(inputs[name])
        arrays[f"in_{name}_dram"] = a
        args.append(nc.dram_tensor(f"in_{name}_dram", a.shape, _mybir.dt.from_np(a.dtype), kind="ExternalInput").ap())
    shape = inputs['L0_attn_y'].shape
    out = nc.dram_tensor("out_0_dram", shape, _mybir.dt.from_np(_np.dtype('float32')), kind="ExternalOutput").ap()
    preln_layer(nc, *args, out)
    r = _run(nc, [arrays], core_ids=[0])
    return r.results[0]["out_0_dram"]
```

```python
from contextlib import ExitStack

import concourse.bass as bass
from concourse import mybir

ALU = mybir.AluOpType
ACT = mybir.ActivationFunctionType
AX = mybir.AxisListType
F32 = mybir.dt.float32
BF16 = mybir.dt.bfloat16
ds = bass.ds

P = 128
EPS = 1e-5

PE_AT = dict(turn_max1=3, proj_k=3, proj_q=9, proj_v=12, turn_max0=18, turn_o=19, prep=22, wo=24)
ACT_AT = dict(hi_k=1, hi_q=6, v_hi=10, o_hi=12, exp=0, stage=1, ln_hi=14)
DVE_AT = dict(row1=1, rden0=1, norm0=4, acc=0, lo_k=1, lo_q=7, v=7, rden1=7, norm1=10, row0=11, o_lo=13, gates0=0,
              gates1=2, gates2=4, gates3=7, gates4=11, x1=14, stats0=0, stats1=2, stats2=6, stats3=7, ln=11,
              ln_lo=15, diff=14)
POOL_AT = dict(v_lo=12, rstd=9)
LAST_ACC, LAST_X1, LAST_STATS, LAST_NORM, LAST_LN = (0, 3), (0, 3), (0, 4), (0, 7), (0, 8)
LAST_ROUTE, LAST_DIFF, LAST_GATES = (1, 5), (1, 6), (1, 8)
LAST_RSTD, LAST_EXP = 5, 8


def preln_layer(nc, y, Wq, bq, Wk, bk, Wv, bv, Wo, bo, s_up, s_dn, r_up, r_dn, r_w, out):
    B, N, D = y.shape
    NE = r_w.shape[0]
    DH = 64
    H = Wq.shape[0] // DH
    PAIRS = H // 2
    HALF = PAIRS // 2
    NB = N // P
    G = 2 * B
    SCALE = float(DH) ** -0.5
    CH = (s_up.shape[0] + NE) // 2
    RC = NE // 2
    TOP = 4
    UN, UB = N // 2, NB // 2
    AHEAD = 6 * UN
    assert D == P and N == 512 and NB == 4 and HALF == 4 and NE == 16 and CH == RC + 1

    CQ, CK, CV, CO = 0, PAIRS, 2 * PAIRS, 3 * PAIRS
    CU = 4 * PAIRS
    CD = CU + CH
    NW = CD + CH

    with ExitStack() as ctx:
        def sb(name, shape, dt):
            return ctx.enter_context(nc.sbuf_tensor(name, shape, dt))

        def pb(name, shape):
            return ctx.enter_context(nc.psum_tensor(name, shape, F32))

        def sem(name):
            return ctx.enter_context(nc.semaphore(name))

        ident = sb("ident", [P, P], F32)
        w_hi = sb("w_hi", [P, NW, P], BF16)
        w_lo = sb("w_lo", [P, NW, P], BF16)
        rw_nat = sb("rw_nat", [NE, P], F32)
        rw_hi = sb("rw_hi", [P, NE], BF16)
        rw_lo = sb("rw_lo", [P, NE], BF16)
        b_nat = sb("b_nat", [2 * PAIRS + 1, P], F32)
        b_col = sb("b_col", [P, 2 * PAIRS + 1], F32)
        bv_row = sb("bv_row", [P, H * DH], F32)
        yT_hi = sb("yT_hi", [P, 22 * N], BF16)
        yT_lo = sb("yT_lo", [P, 22 * N], BF16)
        accT = sb("accT", [P, (B + 1) * N], F32)
        w_nat = accT[:, 0:NW * P].rearrange("p (c n) -> p c n", n=P)
        stack = sb("stack", [P, 4, 8, N], BF16)
        KA0, KB0, KA1, KB1, QA0, QA1, QB0, QB1 = range(8)
        xw = sb("xw", [P, 4, D], F32)
        xn = sb("xn", [P, 4, D], F32)
        acc_st = sb("acc_st", [P, N], F32)
        stats = sb("stats", [P, 4, 6], F32)
        ln = sb("ln", [P, 4, 4], F32)
        mhalf = sb("mhalf", [P, 4], F32)
        rt = sb("rt", [P, 2, NB, NE], F32)
        rrest = sb("rrest", [P, NB, NE + 4], F32)
        rx = sb("rx", [P, NB, NE + 4], F32)
        top8 = sb("top8", [P, NB, 8], F32)
        rsm = sb("rsm", [P, 4, NB], F32)
        gates = sb("gates", [P, G + 3, UB, NE], F32)
        h_stage = sb("h_stage", [P, 2, N], BF16)
        l_stage = sb("l_stage", [P, 2, N], BF16)
        v32 = sb("v32", [P, H // 2 * DH], F32)
        vt = sb("vt", [P, 2, NB, H // 2, 129], BF16)
        mx = sb("mx", [P, 2, 8], F32)
        mrow = sb("mrow", [NB, P], BF16)
        p32 = sb("p32", [P, 4, N], F32)
        p_hi = sb("p_hi", [P, 2, NB, N], BF16)
        p_lo = sb("p_lo", [P, 2, NB, N], BF16)
        rden = sb("rden", [P, 2, NB], F32)
        o_sb = sb("o_sb", [P, NB, P], F32)
        oT_hi = sb("oT_hi", [P, N], BF16)
        oT_lo = sb("oT_lo", [P, N], BF16)

        sel = sb("sel", [P, RC, P], BF16)

        sf = stack[:, :, :, :].rearrange("p a b n -> p (a b n)")
        gateT = sf[:, 0:2 * N].rearrange("p (a n) -> p a n", a=2)
        a_hi = sf[:, 2 * N:5 * N].rearrange("p (a n) -> p a n", a=3)
        a_lo = sf[:, 5 * N:8 * N].rearrange("p (a n) -> p a n", a=3)
        gl = sf[:, 8 * N:14 * N].bitcast(F32).rearrange("p (a n) -> p a n", a=3)
        a32 = sf[:, 14 * N:20 * N].bitcast(F32).rearrange("p (a n) -> p a n", a=3)
        o_st = sf[:, 20 * N:24 * N].bitcast(F32).rearrange("p (a n) -> p a n", a=2)
        f_sb = sf[:, 24 * N:26 * N].bitcast(F32)
        g_st = sf[:, 26 * N:27 * N].bitcast(F32)[:, 0:NB * NE].rearrange("p (t e) -> p t e", e=NE)

        ps_s = pb("ps_s", [P, 2, N])
        ps_z = pb("ps_z", [P, 2, N])
        ps_o = pb("ps_o", [P, 2, N])
        ps_m = pb("ps_m", [P, 2, N])

        names = """ident selz zero wload_q wload_k wload_v wload_o wload_u wload_d bload vload wT w_hi_ok w_lo_ok bT b_ok
            acc_init ones_ok pinit xload var_ok ln_chain rstd_ok xn_ok xT xT_hi_ok xT_lo_ok
            proj hi_ok lo_ok stacked vproj v32_ok vhi_ok vlo_ok smax max_ok mT mrow_ok mrow_in
            scores exp_ok plo_ok pv rden_ok o_ok oT oTh_ok oTl_ok wo acc_ok
            acc_staged accT_turned x1_ok logits diff_ok rexp_ok gate_chain gates_ok
            attn_done g_staged gT gTh_ok gTl_ok up gelu gbc act_ok ah_ok al_ok down f_ok fT out_ok""".split()
        S = {n: sem(n) for n in names}
        x_in = [sem(f"x_in{i}") for i in range(2)]
        st = [sem(f"stored{i}") for i in range(2)]

        block = ctx.enter_context(nc.Block())

        def n_exp(c): return c + 3
        def n_plo(c): return c + 5
        def n_pv(v): return v + 3
        def n_o(v): return v + 4
        def n_wo(x): return x + 3
        def n_acc(x): return x + 3
        def n_oT(x): return x + 2
        STK = 10 * 16

        def n_ln(g): return g + 3
        def n_diff(g): return g + 2
        def n_gelu(k): return k + 3
        def n_al(k): return k + 4
        def n_act(b, c): return b * RC + c + 2

        def two_units(t, g):
            return t[:, ds(g * UN, 2 * AHEAD)].rearrange("p (a n) -> p a n", a=2)[:, :, 0:UN]

        def whole_batch(t, b):
            return t[:, (b + 1) * N:(b + 2) * N].rearrange("p (a n) -> p a n", n=UN)

        tok = "(t p) d -> p t d"
        y_units = y.rearrange("b (h n) d -> (b h) n d", h=2)
        x_first = p32[:, 0:2, :].rearrange("p a (t d) -> p a t d", d=D)
        w_banks = [ps_s[:, 0, :], ps_s[:, 1, :], ps_z[:, 0, :], ps_z[:, 1, :]]

        groups = [(c, min(4, end - c), nm, v)
                  for start, end, nm, v in ((CQ, CK, "wload_q", 16), (CK, CV, "wload_k", 16), (CV, CO, "wload_v", 16),
                                            (CO, CU, "wload_o", 16), (CU, CD, "wload_u", 32), (CD, NW, "wload_d", 32))
                  for c in range(start, end, 4)]
        EARLY = 2 * PAIRS // 4

        @block.sync
        def _(sp):
            def load_w(w, c, name):
                sp.dma_start(w_nat[:, c:c + PAIRS, :], w.rearrange("(c p) d -> p c d", p=P)).then_inc(S[name], 16)

            sp.dma_start(x_first[:, 0, :, :], y[0].rearrange(tok, p=P)).then_inc(x_in[0], 16)
            load_w(Wq, CQ, "wload_q")
            load_w(Wk, CK, "wload_k")
            load_w(Wv, CV, "wload_v")
            sp.dma_start(x_first[:, 1, :, :], y[1].rearrange(tok, p=P)).then_inc(x_in[1], 16)
            sp.dma_start(w_nat[:, CO:CO + PAIRS, :], Wo.rearrange("d (c e) -> d c e", e=P)).then_inc(S["wload_o"], 16)
            sp.dma_start(w_nat[:, CU:CU + 1, :], s_up.rearrange("(c s) e h -> (s e) c h", s=2)).then_inc(S["wload_u"], 16)
            sp.dma_start(w_nat[:, CU + 1:CU + CH, :], r_up.rearrange("(c s) e h -> (s e) c h", s=2)).then_inc(S["wload_u"], 16)
            sp.dma_start(w_nat[:, CD, :].rearrange("h (s e) -> h s e", s=2), s_dn.rearrange("s h e -> h s e")).then_inc(S["wload_d"], 16)
            sp.dma_start(w_nat[:, CD + 1:CD + CH, :].rearrange("h c (s e) -> h (c s) e", s=2),
                         r_dn.rearrange("r h e -> h r e")).then_inc(S["wload_d"], 16)

            def load_units(g):
                for k, u in enumerate(((g + G - 2) % G, (g + 4) % G)):
                    sp.dma_start(xw[:, 2 * k:2 * k + 2, :], y_units[ds(u, 1)].rearrange("o (t p) d -> p (o t) d", p=P)).then_inc(S["xload"], 16)

            def move(t, to, col, n, src, of):
                dst = t[to:to + 64, col:col + n, :]
                sp.dma_start(dst, src[of:of + 64].unsqueeze(1).broadcast_to([64, n, N])).then_inc(S["stacked"], 16)

            def stack_k(x, j):
                h, l, t = h_stage[:, 0, :], l_stage[:, 0, :], stack[:, j, :, :]
                sp.wait_ge(S["hi_ok"], 2 * x + 1)
                move(t, 0, KA0, 2, h, 0)
                move(t, 64, KA1, 2, h, 64)
                sp.wait_ge(S["lo_ok"], 2 * x + 1)
                move(t, 64, KA0, 1, l, 0)
                move(t, 0, KA1, 1, l, 64)

            def stack_q_hi(x, j):
                h, t = h_stage[:, 1, :], stack[:, j, :, :]
                sp.wait_ge(S["hi_ok"], 2 * x + 2)
                for to in (0, 64):
                    move(t, to, QA0, 1, h, 0)
                    move(t, to, QA1, 1, h, 64)

            def stack_q_lo(x, j):
                l, t = l_stage[:, 1, :], stack[:, j, :, :]
                sp.wait_ge(S["lo_ok"], 2 * x + 2)
                move(t, 0, QB0, 1, l, 0)
                move(t, 64, QB1, 1, l, 64)

            def max_row(x, j, h):
                sp.wait_ge(S["mrow_ok"], 2 * x + h + 1)
                dst = stack[64:65, j, QB0, :] if h == 0 else stack[0:1, j, QB1, :]
                sp.dma_start(dst.rearrange("o (t q) -> o t q", q=P), mrow[:, :]).then_inc(S["mrow_in"], 16)

            sp.wait_ge(S["ones_ok"], 2)
            load_units(0)
            for x in range(2):
                stack_k(x, x)
                stack_q_hi(x, x)
                stack_q_lo(x, x)
            max_row(0, 0, 0)
            with sp.Fori(0, G) as g:
                for j in range(HALF):
                    p = g * HALF + j
                    max_row(p, j, 1)
                    stack_k(p + 2, (j + 2) % 4)
                    stack_q_hi(p + 2, (j + 2) % 4)
                    stack_q_lo(p + 2, (j + 2) % 4)
                    max_row(p + 1, (j + 1) % 4, 0)
                    if j == 3:
                        sp.wait_ge(S["xn_ok"], n_ln(g))
                        load_units(g + 1)
            sp.wait_ge(S["xload"], (G + 1) * 32)
            sp.dma_start(xw[:, UB:NB, :], y_units[G - 1].rearrange("(t p) d -> p t d", p=P)).then_inc(S["xload"], 16)

            for par in range(2):
                sp.sem_inc(st[par], 16)
            with sp.Fori(0, B // 2) as i:
                for par in range(2):
                    b = i * 2 + par
                    sp.wait_ge(S["out_ok"], b + 1)
                    sp.dma_start(out[ds(b, 1)].rearrange("o (t p) d -> p (o t) d", p=P),
                                 o_st[:, par, :].rearrange("p (t d) -> p t d", d=D)).then_inc(st[par], 16)
            for par in range(2):
                sp.wait_ge(st[par], 16 * (B // 2 + 1))

        @block.gpsimd
        def _(pool):
            nc.gpsimd.memset(mhalf[:, :], -0.5)
            nc.gpsimd.memset(ident[:, :], 0.0).then_inc(S["ident"], 1)
            pool.wait_ge(S["ident"], 1)
            nc.gpsimd.affine_select(out=ident[:, :], in_=ident[:, :], compare_op=ALU.not_equal, fill=1.0, base=0,
                                    pattern=[[-1, P]], channel_multiplier=1).then_inc(S["ident"], 1)
            def rstd_of(n):
                pool.wait_ge(S["var_ok"], n + 1)
                nc.gpsimd.tensor_tensor(ln[:, 2, :], ln[:, 1, :], mhalf[:, :], ALU.pow).then_inc(S["rstd_ok"], 1)

            rstd_of(0)
            nc.gpsimd.memset(stack[:, :, KB0, :], 0.0)
            nc.gpsimd.memset(stack[:, :, KB1, :], 0.0)
            nc.gpsimd.memset(stack[:, :, QB0:QB1 + 1, :], 0.0).then_inc(S["ones_ok"], 1)
            pool.wait_ge(S["ones_ok"], 1)
            nc.gpsimd.memset(stack[64:65, :, KB0, :], 1.0)
            nc.gpsimd.memset(stack[0:1, :, KB1, :], 1.0).then_inc(S["ones_ok"], 1)
            pool.wait_ge(S["ones_ok"], 2)
            rstd_of(1)
            nc.gpsimd.memset(vt[:, :, :, :, 64:65], 1.0)
            nc.gpsimd.memset(vt[:, 1, :, H // 2 - 1:H // 2, 0:64], 1.0)
            nc.gpsimd.memset(vt[:, 1, :, H // 2 - 1:H // 2, 65:129], 1.0)
            nc.gpsimd.memset(p_hi[:, 1, :, :], 1.0)
            nc.gpsimd.memset(p_lo[:, 1, :, :], 0.0)
            nc.gpsimd.memset(rt[:, 0, :, :], 0.0)
            nc.gpsimd.memset(rx[:, :, NE:NE + 4], -1.0)
            nc.gpsimd.memset(o_sb[:, :, :], 0.0).then_inc(S["pinit"], 1)
            nc.gpsimd.memset(sel[:, :, :], 0.0).then_inc(S["selz"], 1)
            v = sel[:, :, :].rearrange("p c (h l) -> p c h l", h=2)
            for k, base in enumerate((0, -32)):
                pool.wait_ge(S["selz"], k + 1)
                nc.gpsimd.affine_select(out=v, in_=v, compare_op=ALU.not_equal, fill=1.0, base=base,
                                        pattern=[[-2, RC], [-1, 2], [0, 64]], channel_multiplier=1).then_inc(S["selz"], 1)
            pool.sem_inc(S["plo_ok"], 4)


            pool.wait_ge(S["w_lo_ok"], len(groups))
            nc.gpsimd.memset(accT[:, :], 0.0).then_inc(S["acc_init"], 1)

            def v_lo(G1, kc, buf):
                pool.wait_ge(S["vhi_ok"], G1 * NB + kc + 1)
                dst = vt[:, ds(buf, 1), kc, :, :].rearrange("p o h c -> p (o h) c")
                nc.gpsimd.tensor_tensor(dst[:, :, 65:129], v32[:, :].rearrange("p (h c) -> p h c", c=DH),
                                        dst[:, :, 0:64], ALU.subtract).then_inc(S["vlo_ok"], 1)

            for kc in range(NB):
                v_lo(0, kc, 0)
            with pool.Fori(0, G) as g:
                for j in range(HALF):
                    p = g * HALF + j
                    for s in range(8):
                        h, kc = s // 4, s % 4
                        pool.wait_ge(S["exp_ok"], n_exp(p * 8 + s))
                        nc.gpsimd.tensor_tensor(p_lo[:, h, kc, :], p32[:, s % 4, :], p_hi[:, h, kc, :],
                                                ALU.subtract).then_inc(S["plo_ok"], 1)
                        if s == 4:
                            v_lo(g + 1, j, (g + 1) % 2)
                        if j == 2 and s == 2:
                            rstd_of(g + 2)

            pool.wait_ge(S["attn_done"], 1)
            nc.gpsimd.memset(gateT[:, :, :], 0.0).then_inc(S["zero"], 1)
            pool.sem_inc(S["al_ok"], 3)

            def act_lo(b, c):
                pool.wait_ge(S["ah_ok"], b * CH + c + 1)
                nc.gpsimd.tensor_tensor(a_lo[:, c % 3, :], (gl if c == 0 else a32)[:, c % 3, :], a_hi[:, c % 3, :],
                                        ALU.subtract).then_inc(S["al_ok"], 1)

            def experts(b, first=False):
                for c in range(3, CH):
                    act_lo(b, c)
                    if first and c == LAST_RSTD:
                        rstd_of(G + 2)
                for c in range(3):
                    act_lo(b + 1, c)

            for c in range(3):
                act_lo(0, c)
            experts(0, first=True)
            with pool.Fori(1, B) as b:
                experts(b)

        @block.scalar
        def _(act):
            act.dma_start(b_nat[0:PAIRS, :], bq.rearrange("(c p) -> c p", p=P)).then_inc(S["bload"], 16)
            act.dma_start(b_nat[PAIRS:2 * PAIRS, :], bk.rearrange("(c p) -> c p", p=P)).then_inc(S["bload"], 16)
            act.dma_start(b_nat[2 * PAIRS:2 * PAIRS + 1, :], bo.rearrange("(c p) -> c p", p=P)).then_inc(S["bload"], 16)
            act.dma_start(rw_nat[:, :], r_w).then_inc(S["bload"], 16)
            act.dma_start(bv_row[:, :], bv.rearrange("(o n) -> o n", o=1).broadcast_to([P, H * DH])).then_inc(S["vload"], 16)
            act.sem_inc(S["exp_ok"], 2)

            def weights_hi(k):
                c0, n = groups[k][0:2]
                act.wait_ge(S["wT"], k + 1)
                act.activation(w_hi[:, c0:c0 + n, :], w_banks[k % 4][:, 0:n * P], ACT.Copy).then_inc(S["w_hi_ok"], 1)

            def xT_hi(n, dst):
                act.wait_ge(S["xT"], n + 1)
                act.activation(dst, ps_m[:, 1, :].rearrange("p (a n) -> p a n", n=UN), ACT.Copy).then_inc(S["xT_hi_ok"], 1)

            xT_hi(0, whole_batch(yT_hi, 0))
            for k in range(EARLY):
                weights_hi(k)
            act.wait_ge(S["bT"], 1)
            act.activation(b_col[:, :], ps_m[:, 0, 0:2 * PAIRS + 1], ACT.Copy)
            act.activation(rw_hi[:, :], ps_m[:, 1, 0:NE], ACT.Copy).then_inc(S["b_ok"], 1)
            def hi_part(x, which, col):
                act.wait_ge(S["proj"], 2 * x + which + 1)
                act.activation(h_stage[:, which, :], ps_m[:, 0, :], ACT.Identity, bias=b_col[:, col]).then_inc(S["hi_ok"], 1)

            def stage_acc(g, n=UN):
                act.wait_ge(S["acc_ok"], n_acc(g * HALF - 1))
                act.activation(acc_st[:, 0:n], accT[:, ds(g * UN, n)], ACT.Identity,
                               bias=b_col[:, 2 * PAIRS:2 * PAIRS + 1]).then_inc(S["acc_staged"], 1)

            def route_exp(g, nb=UB):
                act.wait_ge(S["diff_ok"], n_diff(g - 1))
                act.activation(rx[:, 0:nb, 0:NE], rt[:, 0, 0:nb, :], ACT.Exp).then_inc(S["rexp_ok"], 1)

            def v_hi(G1, kc, buf):
                act.wait_ge(S["v32_ok"], G1 * NB + kc + 1)
                dst = vt[:, ds(buf, 1), kc, :, 0:64].rearrange("p o h c -> p (o h) c")
                act.activation(dst, v32[:, :].rearrange("p (h c) -> p h c", c=DH), ACT.Copy).then_inc(S["vhi_ok"], 1)

            for which in range(2):
                hi_part(0, which, slice(PAIRS * (1 - which), PAIRS * (1 - which) + 1))
            for k in range(EARLY, len(groups)):
                weights_hi(k)
            act.wait_ge(S["stacked"], STK)
            for which in range(2):
                hi_part(1, which, slice(PAIRS * (1 - which) + 1, PAIRS * (1 - which) + 2))
            xT_hi(1, whole_batch(yT_hi, 1))
            act.wait_ge(S["pinit"], 1)
            for kc in range(NB):
                v_hi(0, kc, 0)
            with act.Fori(0, G) as g:
                for j in range(HALF):
                    p = g * HALF + j
                    col = (g % 2) * HALF + j + 2 if j < 2 else ((g + 1) % 2) * HALF + j - 2
                    for at in range(16):
                        s = at // 2
                        h, kc = s // 4, s % 4
                        c = p * 8 + s
                        if at % 2 == 1:
                            act.wait_ge(S["scores"], c + 1)
                            act.wait_ge(S["plo_ok"], n_plo(c - 4))
                            act.activation(p32[:, s % 4, :], ps_s[:, s % 2, :], ACT.Exp, scale=SCALE)
                            if kc == 0:
                                act.wait_ge(S["pv"], n_pv(p * 2 + h - 2))
                            act.activation(p_hi[:, h, kc, :], ps_s[:, s % 2, :], ACT.Exp, scale=SCALE).then_inc(S["exp_ok"], 1)
                        if at == ACT_AT["hi_k"]:
                            act.wait_ge(S["stacked"], (p + 2) * STK)
                            hi_part(p + 2, 0, ds(col + PAIRS, 1))
                        if at == ACT_AT["hi_q"]:
                            hi_part(p + 2, 1, ds(col, 1))
                        if at == ACT_AT["v_hi"]:
                            act.wait_ge(S["pv"], n_pv(g * 8 - 1))
                            v_hi(g + 1, j, (g + 1) % 2)
                        if at == ACT_AT["o_hi"]:
                            act.wait_ge(S["oT"], n_oT(p - 1))
                            act.wait_ge(S["wo"], n_wo(p - 2))
                            act.activation(oT_hi[:, :], ps_m[:, 0, :], ACT.Copy).then_inc(S["oTh_ok"], 1)
                        if j == 0 and at == ACT_AT["exp"]:
                            route_exp(g)
                        if j == 1 and at == ACT_AT["stage"]:
                            stage_acc(g)
                        if j == 2 and at == ACT_AT["ln_hi"]:
                            xT_hi(g + 2, two_units(yT_hi, g))
            def gate_hi(n, par):
                act.wait_ge(S["gT"], n + 1)
                act.activation(gateT[0:NE, par, :], ps_m[0:NE, 0, :], ACT.Copy).then_inc(S["gTh_ok"], 1)

            def gelu(b, c, par):
                k = b * CH + c
                act.wait_ge(S["up"], k + 1)
                act.wait_ge(S["al_ok"], n_al(k - 3))
                act.activation(gl[:, c % 3, :], ps_s[:, (par + c) % 2, :], ACT.Gelu).then_inc(S["gelu"], 1)

            def experts(b, par, n=None):
                for c in range(3, CH):
                    gelu(b, c, par)
                    if c == 4:
                        gate_hi(b + 1, 1 - par)
                    if n == 1 and c == LAST_EXP:
                        route_exp(G + 1, NB)
                if n == 0:
                    xT_hi(G + 2, whole_batch(yT_hi, B - 1))
                gelu(b + 1, 0, 1 - par)
                gelu(b + 1, 1, 1 - par)
                act.wait_ge(S["down"], (b + 1) * CH)
                act.activation(f_sb, ps_z[:, par, :], ACT.Copy).then_inc(S["f_ok"], 1)
                gelu(b + 1, 2, 1 - par)

            route_exp(G)
            act.wait_ge(S["zero"], 1)
            act.sem_inc(S["gelu"], 2)
            gate_hi(0, 0)
            gelu(0, 0, 0)
            act.wait_ge(S["oT"], n_oT(G * HALF - 1))
            act.activation(oT_hi[:, :], ps_m[:, 0, :], ACT.Copy).then_inc(S["oTh_ok"], 1)
            gelu(0, 1, 0)
            gelu(0, 2, 0)
            stage_acc(G, N)
            for n in range(2):
                experts(n, n, n)
            with act.Fori(1, B // 2) as i:
                for par in range(2):
                    experts(i * 2 + par, par)

        @block.vector
        def _(dve):
            def weights_lo(k):
                c0, n = groups[k][0:2]
                dve.wait_ge(S["w_hi_ok"], k + 1)
                nc.vector.tensor_tensor(w_lo[:, c0:c0 + n, :], w_banks[k % 4][:, 0:n * P].rearrange("p (c n) -> p c n", n=P),
                                        w_hi[:, c0:c0 + n, :], ALU.subtract).then_inc(S["w_lo_ok"], 1)

            def ln_stats(n, src, part):
                if part > 0:
                    dve.wait_ge(S["ln_chain"], n * 3 + part)
                me, qe, mo, qo = (stats[:, :, f] for f in (1, 2, 4, 5))
                mean, var, tmp = ln[:, 0, :], ln[:, 1, :], ln[:, 3, :]
                if part == 0:
                    for t in range(4):
                        ins = nc.vector.bn_stats(stats[:, t, :], src[:, t, :])
                if part == 1:
                    nc.vector.tensor_tensor(mean, me, mo, ALU.add)
                    nc.vector.tensor_tensor(tmp, me, mo, ALU.subtract)
                    ins = nc.vector.tensor_tensor(var, qe, qo, ALU.add)
                if part == 2:
                    nc.vector.tensor_scalar(mean, mean, 0.5, None, ALU.mult)
                    nc.vector.tensor_scalar(var, var, 1.0 / D, EPS, ALU.mult, ALU.add)
                    ins = nc.vector.scalar_tensor_tensor(out=tmp, in0=tmp, scalar=0.25, in1=tmp, op0=ALU.mult, op1=ALU.mult)
                if part < 3:
                    ins.then_inc(S["ln_chain"], 1)
                else:
                    nc.vector.tensor_tensor(var, var, tmp, ALU.add).then_inc(S["var_ok"], 1)

            def ln_norm(n, src):
                dve.wait_ge(S["rstd_ok"], n + 1)
                for t in range(4):
                    ins = nc.vector.tensor_scalar(xn[:, t, :], src[:, t, :], ln[:, 0, t:t + 1], ln[:, 2, t:t + 1],
                                                  ALU.subtract, ALU.mult)
                ins.then_inc(S["xn_ok"], 1)

            def ln_lo(n, lo, hi):
                dve.wait_ge(S["xT_hi_ok"], n + 1)
                nc.vector.tensor_tensor(lo, ps_m[:, 1, :].rearrange("p (a n) -> p a n", n=UN), hi, ALU.subtract).then_inc(S["xT_lo_ok"], 1)

            def wide(m):
                return m.unsqueeze(2).broadcast_to([P, m.shape[1], NE])

            def x1_of(g, nb=UB):
                dve.wait_ge(S["accT_turned"], g + 1)
                dve.wait_ge(S["xload"], (g + 1) * 32 + (0 if nb == UB else 16))
                nc.vector.tensor_tensor(xw[:, 0:nb, :], ps_m[:, 1, 0:nb * P].rearrange("p (t d) -> p t d", d=D), xw[:, 0:nb, :],
                                        ALU.add).then_inc(S["x1_ok"], 1)

            def keep_x1(g, nb=UB):
                dve.wait_ge(S["x1_ok"], g + 1)
                nc.vector.tensor_copy(accT[:, ds(g * UN, nb * P)], xw[:, 0:nb, :].rearrange("p t d -> p (t d)"))

            def route_diff(g, nb=UB):
                lg = ps_m[:, 1, 0:nb * NE].rearrange("p (t e) -> p t e", e=NE)
                dve.wait_ge(S["logits"], g + 1)
                nc.vector.tensor_reduce(rsm[:, 0, 0:nb], lg, AX.X, ALU.max).then_inc(S["gate_chain"], 1)
                dve.wait_ge(S["gate_chain"], g * 5 + 5)
                nc.vector.tensor_tensor(rt[:, 0, 0:nb, :], lg, wide(rsm[:, 0, 0:nb]), ALU.subtract).then_inc(S["diff_ok"], 1)

            def route_gates(g, part, nb=UB):
                if part > 0:
                    dve.wait_ge(S["gate_chain"], g * 5 + part)
                e, rest, top = rx[:, 0:nb, 0:NE], rrest[:, 0:nb, :], rt[:, 1, 0:nb, :]
                if part == 0:
                    dve.wait_ge(S["rexp_ok"], g + 1)
                    nc.vector.tensor_reduce(rsm[:, 1, 0:nb], e, AX.X, ALU.add)
                    for t in range(nb):
                        ins = nc.vector.max(top8[:, t, :], rx[:, t, 0:NE])
                if part == 1:
                    ins = nc.vector.memset(top8[:, 0:nb, TOP:8], -1.0)
                if part == 2:
                    nc.vector.reciprocal(rsm[:, 2, 0:nb], rsm[:, 1, 0:nb])
                    for t in range(nb):
                        ins = nc.vector.match_replace(rest[:, t, :], top8[:, t, :], rx[:, t, :], 0.0)
                if part == 3:
                    ins = nc.vector.tensor_tensor(top, e, rest[:, :, 0:NE], ALU.subtract)
                if part < 4:
                    ins.then_inc(S["gate_chain"], 1)
                else:
                    nc.vector.tensor_tensor(gates[:, ds(g, nb // UB), :, :].rearrange("p o t e -> p (o t) e"), top,
                                            wide(rsm[:, 2, 0:nb]), ALU.mult).then_inc(S["gates_ok"], 1)

            dve.wait_ge(x_in[0], 16)
            for part in range(4):
                ln_stats(0, x_first[:, 0, :, :], part)
            ln_norm(0, x_first[:, 0, :, :])
            ln_lo(0, whole_batch(yT_lo, 0), whole_batch(yT_hi, 0))
            for k in range(EARLY):
                weights_lo(k)
            dve.wait_ge(S["b_ok"], 1)
            nc.vector.tensor_tensor(rw_lo[:, :], ps_m[:, 1, 0:NE], rw_hi[:, :], ALU.subtract).then_inc(S["b_ok"], 1)

            def lo_part(x, which, col):
                dve.wait_ge(S["hi_ok"], 2 * x + which + 1)
                nc.vector.scalar_tensor_tensor(out=l_stage[:, which, :], in0=ps_m[:, 0, :], scalar=b_col[:, col],
                                               in1=h_stage[:, which, :], op0=ALU.add, op1=ALU.subtract).then_inc(S["lo_ok"], 1)

            def v_bias(G1, kc, half, first):
                dve.wait_ge(S["vproj"], G1 * NB + kc + 1)
                if not first:
                    dve.wait_ge(S["vlo_ok"], G1 * NB + kc)
                nc.vector.tensor_tensor(v32[:, :], ps_m[:, 1, :], bv_row[:, ds(half * 512, 512)], ALU.add).then_inc(S["v32_ok"], 1)

            def row_max(x, par, t):
                dve.wait_ge(S["smax"], x * 8 + t + 1)
                nc.vector.tensor_reduce(mx[:, par, t:t + 1], ps_z[:, t % 2, :], AX.X, ALU.max).then_inc(S["max_ok"], 1)

            def max_row(x, h, first=False):
                e = x * 2 + h
                dve.wait_ge(S["mT"], e + 1)
                if not first:
                    dve.wait_ge(S["mrow_in"], e * 16)
                nc.vector.tensor_scalar(mrow[:, :], ps_m[0:NB, 1, 0:P], -1.0, None, ALU.mult).then_inc(S["mrow_ok"], 1)

            def normalise(v, h, part):
                o = ps_o[:, h, 0:NB * 65].rearrange("p (t c) -> p t c", c=65)
                if part == 0:
                    dve.wait_ge(S["pv"], n_pv(v))
                    nc.vector.reciprocal(rden[:, h, :], o[:, :, 64]).then_inc(S["rden_ok"], 1)
                else:
                    dve.wait_ge(S["rden_ok"], v + 3)
                    nc.vector.tensor_tensor(o_sb[:, :, h * 64:h * 64 + 64], o[:, :, 0:64],
                                            rden[:, h, :].unsqueeze(2).broadcast_to([P, NB, 64]), ALU.mult).then_inc(S["o_ok"], 1)

            def o_lo(x):
                dve.wait_ge(S["oTh_ok"], n_oT(x))
                nc.vector.tensor_tensor(oT_lo[:, :], ps_m[:, 0, :], oT_hi[:, :], ALU.subtract).then_inc(S["oTl_ok"], 1)

            def add_wo(x, dst):
                dve.wait_ge(S["wo"], n_wo(x))
                nc.vector.tensor_tensor(dst, ps_m[:, 0, :], dst, ALU.add).then_inc(S["acc_ok"], 1)

            nc.vector.memset(ps_o[:, 0, :], 1.0).then_inc(S["o_ok"], 1)
            for which in range(2):
                lo_part(0, which, slice(PAIRS * (1 - which), PAIRS * (1 - which) + 1))
            for k in range(EARLY, len(groups)):
                weights_lo(k)
                if k == EARLY:
                    dve.wait_ge(x_in[1], 16)
                    dve.wait_ge(S["xT_lo_ok"], 1)
                if k < EARLY + 4:
                    ln_stats(1, x_first[:, 1, :, :], k - EARLY)
                if k == EARLY + 5:
                    ln_norm(1, x_first[:, 1, :, :])
            dve.wait_ge(S["stacked"], STK)
            for which in range(2):
                lo_part(1, which, slice(PAIRS * (1 - which) + 1, PAIRS * (1 - which) + 2))
            ln_lo(1, whole_batch(yT_lo, 1), whole_batch(yT_hi, 1))
            dve.wait_ge(S["vload"], 16)
            for t in range(8):
                if t in (0, 2, 4):
                    v_bias(0, t // 2, 0, t == 0)
                if t == 5:
                    max_row(0, 0, True)
                    v_bias(0, 3, 0, False)
                row_max(0, 0, t)
            dve.sem_inc(S["diff_ok"], 1)
            dve.wait_ge(S["acc_init"], 1)
            with dve.Fori(0, G) as g:
                for j in range(HALF):
                    p = g * HALF + j
                    col = (g % 2) * HALF + j + 2 if j < 2 else ((g + 1) % 2) * HALF + j - 2
                    for at in range(16):
                        s = at // 2
                        if at % 2 == 1:
                            row_max(p + 1, (j + 1) % 2, s)
                        if at == DVE_AT["rden0"]:
                            normalise(p * 2 - 2, 0, 0)
                        if at == DVE_AT["acc"]:
                            to = (g + 1) // 2 if j < 2 else g // 2 + 1
                            add_wo(p - 2, accT[:, ds(to * N, N)])
                        if at == DVE_AT["row1"]:
                            max_row(p, 1)
                        if at == DVE_AT["norm0"]:
                            normalise(p * 2 - 2, 0, 1)
                        if at == DVE_AT["lo_k"]:
                            lo_part(p + 2, 0, ds(col + PAIRS, 1))
                        if at == DVE_AT["lo_q"]:
                            lo_part(p + 2, 1, ds(col, 1))
                        if at == DVE_AT["v"]:
                            v_bias(g + 1, j, (g + 1) % 2, False)
                        if at == DVE_AT["rden1"]:
                            normalise(p * 2 - 1, 1, 0)
                        if at == DVE_AT["row0"]:
                            max_row(p + 1, 0)
                        if at == DVE_AT["norm1"]:
                            normalise(p * 2 - 1, 1, 1)
                        if at == DVE_AT["o_lo"]:
                            o_lo(p - 1)
                        if j == 0:
                            for part in range(5):
                                if at == DVE_AT[f"gates{part}"]:
                                    route_gates(g, part)
                        if j == 1 and at == DVE_AT["x1"]:
                            x1_of(g)
                        if j == 2:
                            if at == DVE_AT["stats0"]:
                                keep_x1(g)
                            for part in range(4):
                                if at == DVE_AT[f"stats{part}"]:
                                    ln_stats(g + 2, xw, part)
                        if j == 2 and at == DVE_AT["ln"]:
                            ln_norm(g + 2, xw)
                        if j == 2 and at == DVE_AT["ln_lo"]:
                            ln_lo(g + 2, two_units(yT_lo, g), two_units(yT_hi, g))
                        if j == 3 and at == DVE_AT["diff"]:
                            route_diff(g)
            LAST = G * HALF - 1
            for part in range(2):
                normalise(2 * LAST, 0, part)
            add_wo(LAST - 1, accT[:, B * N:(B + 1) * N])

            def stage_gates(n, b):
                nc.vector.tensor_copy(g_st, gates[:, ds(b * 2 + 3, 2), :, :].rearrange("p u t e -> p (u t) e")).then_inc(S["g_staged"], 1)

            def gate_lo(n, par):
                dve.wait_ge(S["gTh_ok"], n + 1)
                nc.vector.tensor_tensor(gateT[32:32 + NE, par, :], ps_m[0:NE, 0, :], gateT[0:NE, par, :],
                                        ALU.subtract).then_inc(S["gTl_ok"], 1)

            def activate(b, c):
                k = b * CH + c
                dve.wait_ge(S["gelu"], n_gelu(k))
                src = gl[:, 0, :]
                if c > 0:
                    dve.wait_ge(S["gbc"], b * RC + c)
                    src = a32[:, c % 3, :]
                    nc.vector.tensor_tensor(src, gl[:, c % 3, :], ps_o[:, c % 2, :], ALU.mult).then_inc(S["act_ok"], 1)
                    dve.wait_ge(S["act_ok"], n_act(b, c))
                nc.vector.tensor_copy(a_hi[:, c % 3, :], src).then_inc(S["ah_ok"], 1)

            def experts(b, par, n=None):
                for c in range(3, CH):
                    activate(b, c)
                    if c == 3:
                        stage_gates(b + 1, (b + 1) % B)
                    if c == 5:
                        gate_lo(b + 1, 1 - par)
                    at = None if n is None else (n, c)
                    if at == LAST_X1:
                        x1_of(G, NB)
                    if at == LAST_STATS:
                        keep_x1(G, NB)
                        for part in range(4):
                            ln_stats(G + 2, xw, part)
                    if at == LAST_NORM:
                        ln_norm(G + 2, xw)
                    if at == LAST_DIFF:
                        route_diff(G, NB)
                    if at == LAST_GATES:
                        route_gates(G + 1, 0, NB)
                        route_gates(G + 1, 1, NB)
                activate(b + 1, 0)
                if n == 0:
                    ln_lo(G + 2, whole_batch(yT_lo, B - 1), whole_batch(yT_hi, B - 1))
                if n == 1:
                    route_gates(G + 1, 2, NB)
                activate(b + 1, 1)
                if n == 1:
                    route_gates(G + 1, 3, NB)
                activate(b + 1, 2)
                if n == 1:
                    route_gates(G + 1, 4, NB)
                dve.wait_ge(S["fT"], b + 1)
                dve.wait_ge(st[par], (b // 2 + 1) * 16)
                nc.vector.tensor_tensor(o_st[:, par, :], ps_m[:, 1, :], accT[:, ds((b + 1) * N, N)], ALU.add).then_inc(S["out_ok"], 1)

            dve.sem_inc(S["act_ok"], 2)
            dve.wait_ge(S["attn_done"], 1)
            dve.wait_ge(S["gates_ok"], G)
            stage_gates(0, 0)
            gate_lo(0, 0)
            for part in range(2):
                normalise(2 * LAST + 1, 1, part)
            activate(0, 0)
            o_lo(LAST)
            activate(0, 1)
            activate(0, 2)
            add_wo(LAST, accT[:, B * N:(B + 1) * N])
            for part in range(5):
                route_gates(G, part)
            for n in range(2):
                experts(n, n, n)
            dve.wait_ge(S["gates_ok"], G + 2)
            with dve.Fori(1, B // 2) as i:
                for par in range(2):
                    experts(i * 2 + par, par)

        @block.tensor
        def _(pe):
            mm, tr = nc.tensor.matmul, nc.tensor.transpose

            def one(ap):
                return ap.rearrange("p o n -> p (o n)")

            pe.wait_ge(S["ident"], 2)
            def turn_weights(k):
                c0, n, nm, v = groups[k]
                pe.wait_ge(S[nm], v)
                if k >= 4:
                    pe.wait_ge(S["w_lo_ok"], k - 3)
                for q in range(n):
                    ins = tr(w_banks[k % 4][:, q * P:(q + 1) * P], w_nat[:, c0 + q, :], ident[:, :])
                ins.then_inc(S["wT"], 1)

            def turn_ln(n):
                pe.wait_ge(S["xn_ok"], n + 1)
                for t in range(4):
                    ins = tr(ps_m[:, 1, t * P:(t + 1) * P], xn[:, t, :], ident[:, :])
                ins.then_inc(S["xT"], 1)

            turn_ln(0)
            for k in range(EARLY):
                turn_weights(k)
            pe.wait_ge(S["bload"], 64)
            pe.wait_ge(S["xT_lo_ok"], 1)
            tr(ps_m[:, 0, 0:2 * PAIRS + 1], b_nat[:, :], ident[0:2 * PAIRS + 1, 0:2 * PAIRS + 1])
            tr(ps_m[:, 1, 0:NE], rw_nat[:, :], ident[0:NE, 0:NE]).then_inc(S["bT"], 1)

            def three(dst, wh, wl, mh, ml):
                mm(dst, wh, mh, start=True, stop=False)
                mm(dst, wl, mh, start=False, stop=False)
                return mm(dst, wh, ml, start=False, stop=True)

            def project(chunk, yb):
                three(ps_m[:, 0, :], one(w_hi[:, ds(chunk, 1), :]), one(w_lo[:, ds(chunk, 1), :]),
                      yT_hi[:, ds(yb * N + N, N)], yT_lo[:, ds(yb * N + N, N)]).then_inc(S["proj"], 1)

            def project_v(half, yb, kc):
                yh = yT_hi[:, ds(yb * N + (N + kc * P), P)]
                yl = yT_lo[:, ds(yb * N + (N + kc * P), P)]
                wh = w_hi[:, ds(half * HALF + CV, HALF), :].rearrange("p c n -> p (c n)")
                wl = w_lo[:, ds(half * HALF + CV, HALF), :].rearrange("p c n -> p (c n)")
                d = ps_m[:, 1, :]
                mm(d, yh, wh, start=True, stop=False)
                mm(d, yh, wl, start=False, stop=False)
                mm(d, yl, wh, start=False, stop=True).then_inc(S["vproj"], 1)

            def queries_scores(j, t):
                ka, qa = ((KA0, QA0), (KA1, QA1))[t // 4]
                q0 = (t % 4) * P
                mm(ps_z[:, t % 2, :], stack[:, j, qa, q0:q0 + P], stack[:, j, ka, :], start=True, stop=True).then_inc(S["smax"], 1)

            def turn_maxima(par, h):
                tr(ps_m[0:NB, 1, 0:P], mx[:, par, 4 * h:4 * h + 4], ident[:, :]).then_inc(S["mT"], 1)

            def pv_chunk(buf, hv, kc, h8):
                for t in range(NB):
                    q = slice(t * P, (t + 1) * P)
                    ph, pl = p_hi[:, hv, kc, q], p_lo[:, hv, kc, q]
                    vh = vt[:, ds(buf, 1), kc, h8, 0:65]
                    vl = vt[:, ds(buf, 1), kc, h8, 65:129]
                    d = ps_o[:, hv, t * 65:t * 65 + 65]
                    mm(d, ph, vh, start=(kc == 0 and t == 0), stop=False, skip_group_check=True)
                    mm(d[:, 0:64], ph, vl, start=False, stop=False, skip_group_check=True)
                    ins = mm(d, pl, vh, start=False, stop=(kc == NB - 1 and t == NB - 1), skip_group_check=True)
                return ins

            def turn_o():
                for t in range(NB):
                    ins = tr(ps_m[:, 0, t * P:(t + 1) * P], o_sb[:, t, :], ident[:, :])
                ins.then_inc(S["oT"], 1)

            def out_proj(chunk):
                three(ps_m[:, 0, :], one(w_hi[:, ds(chunk, 1), :]), one(w_lo[:, ds(chunk, 1), :]),
                      oT_hi[:, :], oT_lo[:, :]).then_inc(S["wo"], 1)

            def turn_acc(g, nb=UB):
                pe.wait_ge(S["acc_staged"], g + 1)
                for t in range(nb):
                    ins = tr(ps_m[:, 1, t * P:(t + 1) * P], acc_st[:, t * P:(t + 1) * P], ident[:, :])
                ins.then_inc(S["accT_turned"], 1)

            def route(g, nb=UB):
                pe.wait_ge(S["xT_lo_ok"], n_ln(g))
                for t in range(nb):
                    xh, xl = (v[:, ds(g * UN + t * P, P)] for v in (yT_hi, yT_lo))
                    d = ps_m[:, 1, t * NE:(t + 1) * NE]
                    mm(d, xh, rw_hi[:, :], start=True, stop=False)
                    mm(d, xh, rw_lo[:, :], start=False, stop=False)
                    ins = mm(d, xl, rw_hi[:, :], start=False, stop=True)
                ins.then_inc(S["logits"], 1)

            pe.wait_ge(S["b_ok"], 2)
            for which in range(2):
                if which > 0:
                    pe.wait_ge(S["lo_ok"], 1)
                project(PAIRS * (1 - which), 0)
            for k in range(EARLY, len(groups)):
                turn_weights(k)
            for which in range(2):
                pe.wait_ge(S["lo_ok"], 2 + which)
                project(PAIRS * (1 - which) + 1, 0)
            turn_ln(1)
            pe.wait_ge(S["w_lo_ok"], len(groups))
            pe.wait_ge(S["stacked"], STK)
            pe.wait_ge(S["xT_lo_ok"], 2)
            for t in range(8):
                if t in (0, 2, 4, 6):
                    if t > 0:
                        pe.wait_ge(S["v32_ok"], t // 2)
                    if t == 6:
                        pe.wait_ge(S["max_ok"], 4)
                        turn_maxima(0, 0)
                        pe.wait_ge(S["mrow_ok"], 1)
                    project_v(0, 0, t // 2)
                if t > 1:
                    pe.wait_ge(S["max_ok"], t - 1)
                queries_scores(0, t)
            pe.wait_ge(S["v32_ok"], NB)
            pe.wait_ge(S["pinit"], 1)
            pe.sem_inc(S["pv"], 1)
            pe.sem_inc(S["wo"], 1)
            with pe.Fori(0, G) as g:
                for j in range(HALF):
                    p = g * HALF + j
                    if j < 2:
                        chunk, yb = (g % 2) * HALF + j + 2, g // 2
                    else:
                        chunk, yb = ((g + 1) % 2) * HALF + j - 2, (g + 1) // 2
                    v = p * 2 - 1
                    for at in range(1, 25):
                        s, step = (at - 1) // 3, (at - 1) % 3
                        h, kc = s // 4, s % 4
                        if step == 0:
                            ka, qa, kb, qb = ((KA0, QA0, KB0, QB0), (KA1, QA1, KB1, QB1))[h]
                            kk = slice(kc * P, (kc + 1) * P)
                            pe.wait_ge(S["exp_ok"], n_exp(p * 8 + s - 2))
                            mm(ps_s[:, s % 2, :], stack[:, j, ka, kk], stack[:, j, qa, :], start=True, stop=False)
                            if kc == 0:
                                pe.wait_ge(S["mrow_in"], (p * 2 + h + 1) * 16)
                            mm(ps_s[:, s % 2, :], stack[:, j, kb, kk], stack[:, j, qb, :], start=False, stop=True).then_inc(S["scores"], 1)
                        if step == 1:
                            if s == 0:
                                pe.wait_ge(S["stacked"], (p + 2) * STK)
                            pe.wait_ge(S["max_ok"], (p + 1) * 8 + s - 1)
                            queries_scores((j + 1) % 4, s)
                        if step == 2:
                            if kc == 0:
                                pe.wait_ge(S["o_ok"], n_o(v + h - 2))
                            if j == 0 and s == 4:
                                pe.wait_ge(S["vlo_ok"], (g + 1) * NB)
                            pe.wait_ge(S["plo_ok"], n_plo((v + h) * 4 + kc))
                            buf = (g + 1) % 2 if j == 0 and h == 0 else g % 2
                            ins = pv_chunk(buf, 1 - h, kc, (2 * j + h - 1) % 8)
                            if kc == NB - 1:
                                ins.then_inc(S["pv"], 1)
                        if at == PE_AT["turn_max1"]:
                            if j == 0:
                                pe.wait_ge(S["diff_ok"], n_diff(g - 1))
                            if j == 2:
                                pe.wait_ge(S["x1_ok"], g + 1)
                            if j == 3:
                                pe.wait_ge(S["xT_lo_ok"], n_ln(g))
                            pe.wait_ge(S["max_ok"], p * 8 + 8)
                            pe.wait_ge(S["mrow_ok"], p * 2 + 1)
                            turn_maxima(j % 2, 1)
                        if at == PE_AT["proj_k"]:
                            pe.wait_ge(S["acc_ok"], n_acc(p - 2))
                            project(chunk + PAIRS, yb)
                        if at == PE_AT["proj_q"]:
                            pe.wait_ge(S["lo_ok"], (p + 2) * 2 + 1)
                            project(chunk, yb)
                        if at == PE_AT["proj_v"]:
                            pe.wait_ge(S["mrow_ok"], p * 2 + 2)
                            if j == 0:
                                pe.wait_ge(S["xT_lo_ok"], g + 1)
                            project_v((g + 1) % 2, (g + 1) // 2, j)
                        if at == PE_AT["turn_max0"]:
                            pe.wait_ge(S["max_ok"], p * 8 + 12)
                            pe.wait_ge(S["v32_ok"], g * NB + NB + j + 1)
                            turn_maxima((j + 1) % 2, 0)
                        if at == PE_AT["turn_o"]:
                            pe.wait_ge(S["o_ok"], n_o(p * 2 - 1))
                            pe.wait_ge(S["lo_ok"], (p + 2) * 2 + 2)
                            turn_o()
                        if at == PE_AT["prep"] and j > 0:
                            pe.wait_ge(S["mrow_ok"], p * 2 + 3)
                            if j == 1:
                                turn_acc(g)
                            elif j == 2:
                                turn_ln(g + 2)
                            else:
                                route(g)
                        if at == PE_AT["wo"]:
                            pe.wait_ge(S["oTl_ok"], n_oT(p - 1))
                            out_proj(((g + 1) % 2) * HALF + (HALF - 1) + CO if j == 0 else (g % 2) * HALF + j - 1 + CO)
            LAST = G * HALF - 1
            pe.wait_ge(S["max_ok"], (LAST + 2) * 8)
            pe.wait_ge(S["vlo_ok"], (G + 1) * NB)
            pe.wait_ge(S["mrow_in"], (LAST * 2 + 3) * 16)
            pe.wait_ge(S["stacked"], (LAST + 3) * STK)
            pe.sem_inc(S["attn_done"], 1)

            def up(b, c, par, yb):
                pe.wait_ge(S["gelu"], n_gelu(b * CH + c - 2))
                x = (yb + 1) * N
                three(ps_s[:, (par + c) % 2, :], w_hi[:, CU + c, :], w_lo[:, CU + c, :],
                      yT_hi[:, ds(x, N)], yT_lo[:, ds(x, N)]).then_inc(S["up"], 1)
                if c > 0:
                    pe.wait_ge(S["act_ok"], n_act(b, c - 2))
                    mm(ps_o[:, c % 2, :], sel[:, c - 1, :], gateT[:, par, :], start=True, stop=True).then_inc(S["gbc"], 1)

            def down(b, c, par):
                pe.wait_ge(S["al_ok"], n_al(b * CH + c))
                w, d = CD + c, ps_z[:, par, :]
                mm(d, w_hi[:, w, :], a_hi[:, c % 3, :], start=(c == 0), stop=False)
                mm(d, w_lo[:, w, :], a_hi[:, c % 3, :], start=False, stop=False)
                mm(d, w_hi[:, w, :], a_lo[:, c % 3, :], start=False, stop=(c == CH - 1)).then_inc(S["down"], 1)

            def turn_gates(n):
                pe.wait_ge(S["g_staged"], n + 1)
                for t in range(NB):
                    ins = tr(ps_m[0:NE, 0, t * P:(t + 1) * P], g_st[:, t, :], ident[:, :])
                ins.then_inc(S["gT"], 1)

            def experts(b, par, nxt, n=None):
                down(b, 0, par)
                for c in range(3, CH):
                    up(b, c, par, b)
                    down(b, c - 2, par)
                    if c == 4:
                        turn_gates(b + 1)
                    at = None if n is None else (n, c)
                    if at == LAST_ACC:
                        turn_acc(G, NB)
                    if at == LAST_LN:
                        pe.wait_ge(S["x1_ok"], G + 1)
                        turn_ln(G + 2)
                    if at == LAST_ROUTE:
                        pe.wait_ge(S["out_ok"], 1)
                        route(G, NB)
                pe.wait_ge(S["gTl_ok"], b + 2)
                up(b + 1, 0, 1 - par, nxt)
                down(b, CH - 2, par)
                up(b + 1, 1, 1 - par, nxt)
                down(b, CH - 1, par)
                up(b + 1, 2, 1 - par, nxt)
                if n == 0:
                    pe.wait_ge(S["xT_lo_ok"], n_ln(G))
                if n == 1:
                    pe.wait_ge(S["diff_ok"], n_diff(G))
                pe.wait_ge(S["f_ok"], b + 1)
                for t in range(NB):
                    ins = tr(ps_m[:, 1, t * P:(t + 1) * P], f_sb[:, t * P:(t + 1) * P], ident[:, :])
                ins.then_inc(S["fT"], 1)

            pe.wait_ge(S["acc_ok"], n_acc(LAST - 1))
            turn_gates(0)
            pe.wait_ge(S["o_ok"], n_o(2 * LAST - 1))
            for kc in range(NB):
                pe.wait_ge(S["plo_ok"], n_plo((2 * LAST + 1) * 4 + kc))
                ins = pv_chunk((G - 1) % 2, 1, kc, 7)
            ins.then_inc(S["pv"], 1)
            up(0, 0, 0, 0)
            pe.wait_ge(S["o_ok"], n_o(2 * LAST + 1))
            pe.wait_ge(S["gTl_ok"], 1)
            turn_o()
            up(0, 1, 0, 0)
            pe.wait_ge(S["oTl_ok"], n_oT(LAST))
            out_proj(CO + PAIRS - 1)
            up(0, 2, 0, 0)
            pe.wait_ge(S["diff_ok"], n_diff(G - 1))
            for n in range(2):
                experts(n, n, n + 1, n)
            with pe.Fori(1, B // 2) as i:
                for par in range(2):
                    b = i * 2 + par
                    experts(b, par, (b + 1) % B)


_INS = ['L0_attn_y', 'L0_attn_Wq', 'L0_attn_bq', 'L0_attn_Wk', 'L0_attn_bk', 'L0_attn_Wv', 'L0_attn_bv', 'L0_attn_Wo',
        'L0_attn_bo', 'L0_ffn_shared_up', 'L0_ffn_shared_down', 'L0_ffn_routed_up', 'L0_ffn_routed_down', 'L0_ffn_router_w']


def kernel(**inputs):
    import numpy as _np
    import concourse.bacc as _bacc
    from concourse import mybir as _mybir
    from concourse.bass_utils import run_bass_kernel_spmd as _run

    nc = _bacc.Bacc("TRN2", target_bir_lowering=False, num_devices=1)
    arrays, args = {}, []
    for name in _INS:
        a = _np.ascontiguousarray(inputs[name])
        arrays[f"in_{name}_dram"] = a
        args.append(nc.dram_tensor(f"in_{name}_dram", a.shape, _mybir.dt.from_np(a.dtype), kind="ExternalInput").ap())
    shape = inputs['L0_attn_y'].shape
    out = nc.dram_tensor("out_0_dram", shape, _mybir.dt.from_np(_np.dtype('float32')), kind="ExternalOutput").ap()
    preln_layer(nc, *args, out)
    r = _run(nc, [arrays], core_ids=[0])
    return r.results[0]["out_0_dram"]
```
